# Optimizing a Trainium2 kernel written in Bass

```python
import numpy as np
import jax
import jax.numpy as jnp

def _softmax(x, axis=-1):
    return jax.nn.softmax(x, axis=axis)

def _gelu(x):
    return jax.nn.gelu(x, approximate=True)

def _silu(x):
    return jax.nn.silu(x)

def _sigmoid(x):
    return jax.nn.sigmoid(x)

def _layernorm(x, axis=-1, eps=1e-05):
    m = jnp.mean(x, axis=axis, keepdims=True)
    v = jnp.var(x, axis=axis, keepdims=True)
    return (x - m) / jnp.sqrt(v + eps)

def _scatter_add(tgt, idx, src, axis=0):
    return tgt.at[idx].add(src)

def _segment_sum(src, seg, n):
    return jax.ops.segment_sum(src, seg, n)
kernel_name = 'mk_seq_preln_d1_jaxref_r8_e315f4'

def setup_inputs(seed: int=0):
    np.random.seed(seed)
    _w = jnp.asarray

    def _L0_attn_setup():
        import jax, jax.numpy as jnp
        import numpy as np
        B, T, D_MODEL = (2, 64, 128)
        D_INNER, D_HEAD, D_CONV = (256, 64, 4)
        N_HEADS, D_STATE = (32, 32)
        DT_MIN, DT_MAX, K_MAX, EPS = (0.0001, 0.1, 0.5, 1e-08)

        def _forward(x, W_in, dw_weight, dw_bias, W_bc, W_out, skip, A_log, dt_bias):
            Bsz, Tlen, D = x.shape
            DI, K = dw_weight.shape
            H, N = A_log.shape
            DH = DI // H
            proj = jnp.einsum('btd,od->bto', x, W_in)
            gate = proj[..., :DI]
            value_raw = proj[..., DI:2 * DI]
            params = proj[..., 2 * DI:].reshape(Bsz, Tlen, H, 2)
            xp = jnp.pad(value_raw, ((0, 0), (K - 1, 0), (0, 0)))
            conv = dw_bias + sum((xp[:, k:k + Tlen, :] * dw_weight[:, k] for k in range(K)))
            value = jax.nn.silu(conv)
            dt = jnp.clip(jax.nn.softplus(params[..., 0] + dt_bias), DT_MIN, DT_MAX)
            kd = K_MAX * jax.nn.sigmoid(params[..., 1])
            A = jnp.exp(A_log)
            bc = jnp.einsum('bti,oi->bto', value, W_bc).reshape(Bsz, Tlen, H, 4, N)
            bc = bc / (jnp.sqrt(jnp.sum(bc * bc, axis=-1, keepdims=True)) + EPS)
            Bz, Bx, Cz, Cx = (bc[..., 0, :], bc[..., 1, :], bc[..., 2, :], bc[..., 3, :])
            u = value.reshape(Bsz, Tlen, H, DH)

            def step(carry, inp):
                z, s = carry
                u_t, dt_t, k_t, Bz_t, Bx_t, Cz_t, Cx_t = inp
                dtE = dt_t[:, :, None, None]
                S = 1.0 / (1.0 + dt_t[..., None] * k_t[..., None] + (dt_t * dt_t)[..., None] * A)
                z = S[..., None] * (z - dtE * A[None, :, :, None] * s + dtE * (Bz_t[..., None] * u_t[:, :, None, :]))
                s = s + dtE * z + dtE * (Bx_t[..., None] * u_t[:, :, None, :])
                y = jnp.einsum('bhn,bhnd->bhd', Cz_t, z) + jnp.einsum('bhn,bhnd->bhd', Cx_t, s)
                return ((z, s), y)
            tm = lambda a: jnp.moveaxis(a, 1, 0)
            init = (jnp.zeros((Bsz, H, N, DH), x.dtype), jnp.zeros((Bsz, H, N, DH), x.dtype))
            _, ys = jax.lax.scan(step, init, (tm(u), tm(dt), tm(kd), tm(Bz), tm(Bx), tm(Cz), tm(Cx)))
            y = jnp.moveaxis(ys, 0, 1).reshape(Bsz, Tlen, DI)
            y = (y + skip * value) * jax.nn.silu(gate)
            return jnp.einsum('bti,oi->bto', y, W_out)
        key = jax.random.key(seed)
        ks = jax.random.split(key, 8)
        n = lambda k, sh, s=1.0: jax.random.normal(k, sh, jnp.float32) * s
        return {'x': n(ks[0], (B, T, D_MODEL)), 'W_in': n(ks[1], (2 * D_INNER + N_HEADS * 2, D_MODEL), D_MODEL ** (-0.5)), 'dw_weight': n(ks[2], (D_INNER, D_CONV), D_CONV ** (-0.5)), 'dw_bias': n(ks[3], (D_INNER,), 0.1), 'W_bc': n(ks[4], (N_HEADS * 4 * D_STATE, D_INNER), D_INNER ** (-0.5)), 'W_out': n(ks[5], (D_MODEL, D_INNER), D_INNER ** (-0.5)), 'skip': jnp.ones((D_INNER,), jnp.float32), 'A_log': n(ks[6], (N_HEADS, D_STATE), 0.5), 'dt_bias': n(ks[7], (N_HEADS,), 0.5)}
    _L0_attn_in = _L0_attn_setup()

    def _L0_ffn_setup():
        import jax, jax.numpy as jnp
        import numpy as np
        LORA_DIM = 16
        LORA_TOKEN_INDEX = 1
        B, S, D, H = (4, 256, 128, 512)
        key = jax.random.key(seed)
        ks = jax.random.split(key, 6)
        x = jax.random.normal(ks[0], (B, S, D), dtype=jnp.float32)
        W1 = jax.random.normal(ks[1], (H, D), dtype=jnp.float32) * 0.02
        b1 = jnp.zeros((H,), dtype=jnp.float32)
        W2 = jax.random.normal(ks[2], (D, H), dtype=jnp.float32) * 0.02
        b2 = jnp.zeros((D,), dtype=jnp.float32)
        scale = jnp.asarray(0.001, dtype=jnp.float32)
        return {'x': x, 'W1': W1, 'b1': b1, 'W2': W2, 'b2': b2, 'scale': scale}
    _L0_ffn_in = _L0_ffn_setup()
    _d = {'L0_attn_x': _L0_attn_in['x'], 'L0_attn_W_in': _L0_attn_in['W_in'], 'L0_attn_dw_weight': _L0_attn_in['dw_weight'], 'L0_attn_dw_bias': _L0_attn_in['dw_bias'], 'L0_attn_W_bc': _L0_attn_in['W_bc'], 'L0_attn_W_out': _L0_attn_in['W_out'], 'L0_attn_skip': _L0_attn_in['skip'], 'L0_attn_A_log': _L0_attn_in['A_log'], 'L0_attn_dt_bias': _L0_attn_in['dt_bias'], 'L0_ffn_W1': _L0_ffn_in['W1'], 'L0_ffn_b1': _L0_ffn_in['b1'], 'L0_ffn_W2': _L0_ffn_in['W2'], 'L0_ffn_b2': _L0_ffn_in['b2'], 'L0_ffn_scale': _L0_ffn_in['scale']}
    _x0 = _d['L0_attn_x']
    _d['L0_attn_x'] = jax.random.normal(jax.random.fold_in(jax.random.key(seed), 1), (1, 2048, 128), dtype=_x0.dtype)
    del _x0
    return _d

def reference(L0_attn_x, L0_attn_W_in, L0_attn_dw_weight, L0_attn_dw_bias, L0_attn_W_bc, L0_attn_W_out, L0_attn_skip, L0_attn_A_log, L0_attn_dt_bias, L0_ffn_W1, L0_ffn_b1, L0_ffn_W2, L0_ffn_b2, L0_ffn_scale):

    def _L0_attn_ref(x, W_in, dw_weight, dw_bias, W_bc, W_out, skip, A_log, dt_bias):
        import jax, jax.numpy as jnp
        import numpy as np
        B, T, D_MODEL = (2, 64, 128)
        D_INNER, D_HEAD, D_CONV = (256, 64, 4)
        N_HEADS, D_STATE = (32, 32)
        DT_MIN, DT_MAX, K_MAX, EPS = (0.0001, 0.1, 0.5, 1e-08)

        def _forward(x, W_in, dw_weight, dw_bias, W_bc, W_out, skip, A_log, dt_bias):
            Bsz, Tlen, D = x.shape
            DI, K = dw_weight.shape
            H, N = A_log.shape
            DH = DI // H
            proj = jnp.einsum('btd,od->bto', x, W_in)
            gate = proj[..., :DI]
            value_raw = proj[..., DI:2 * DI]
            params = proj[..., 2 * DI:].reshape(Bsz, Tlen, H, 2)
            xp = jnp.pad(value_raw, ((0, 0), (K - 1, 0), (0, 0)))
            conv = dw_bias + sum((xp[:, k:k + Tlen, :] * dw_weight[:, k] for k in range(K)))
            value = jax.nn.silu(conv)
            dt = jnp.clip(jax.nn.softplus(params[..., 0] + dt_bias), DT_MIN, DT_MAX)
            kd = K_MAX * jax.nn.sigmoid(params[..., 1])
            A = jnp.exp(A_log)
            bc = jnp.einsum('bti,oi->bto', value, W_bc).reshape(Bsz, Tlen, H, 4, N)
            bc = bc / (jnp.sqrt(jnp.sum(bc * bc, axis=-1, keepdims=True)) + EPS)
            Bz, Bx, Cz, Cx = (bc[..., 0, :], bc[..., 1, :], bc[..., 2, :], bc[..., 3, :])
            u = value.reshape(Bsz, Tlen, H, DH)

            def step(carry, inp):
                z, s = carry
                u_t, dt_t, k_t, Bz_t, Bx_t, Cz_t, Cx_t = inp
                dtE = dt_t[:, :, None, None]
                S = 1.0 / (1.0 + dt_t[..., None] * k_t[..., None] + (dt_t * dt_t)[..., None] * A)
                z = S[..., None] * (z - dtE * A[None, :, :, None] * s + dtE * (Bz_t[..., None] * u_t[:, :, None, :]))
                s = s + dtE * z + dtE * (Bx_t[..., None] * u_t[:, :, None, :])
                y = jnp.einsum('bhn,bhnd->bhd', Cz_t, z) + jnp.einsum('bhn,bhnd->bhd', Cx_t, s)
                return ((z, s), y)
            tm = lambda a: jnp.moveaxis(a, 1, 0)
            init = (jnp.zeros((Bsz, H, N, DH), x.dtype), jnp.zeros((Bsz, H, N, DH), x.dtype))
            _, ys = jax.lax.scan(step, init, (tm(u), tm(dt), tm(kd), tm(Bz), tm(Bx), tm(Cz), tm(Cx)))
            y = jnp.moveaxis(ys, 0, 1).reshape(Bsz, Tlen, DI)
            y = (y + skip * value) * jax.nn.silu(gate)
            return jnp.einsum('bti,oi->bto', y, W_out)
        return _forward(x, W_in, dw_weight, dw_bias, W_bc, W_out, skip, A_log, dt_bias)

    def _L0_ffn_ref(x, W1, b1, W2, b2, scale):
        import jax, jax.numpy as jnp
        import numpy as np
        LORA_DIM = 16
        LORA_TOKEN_INDEX = 1
        B, S, D, H = (4, 256, 128, 512)
        Bx, Sx, Dx = x.shape
        Hx = W1.shape[0]
        lt = jax.lax.dynamic_slice_in_dim(x, LORA_TOKEN_INDEX, LORA_DIM, axis=1)
        even = lt[:, ::2, :]
        odd = lt[:, 1::2, :]
        m1 = (even[:, :4, :, None] * odd[:, :4, None, :]).reshape(Bx, Hx, Dx)
        m2 = (even[:, 4:, :, None] * odd[:, 4:, None, :]).reshape(Bx, Dx, Hx)
        h = jnp.einsum('bsd,hd->bsh', x, W1) + scale * jnp.einsum('bsd,bhd->bsh', x, m1) + b1
        h = jax.nn.gelu(h, approximate=False)
        out = jnp.einsum('bsh,oh->bso', h, W2) + scale * jnp.einsum('bsh,boh->bso', h, m2) + b2
        return out
    x = L0_attn_x
    x = x + _L0_attn_ref(_layernorm(x, axis=-1), L0_attn_W_in, L0_attn_dw_weight, L0_attn_dw_bias, L0_attn_W_bc, L0_attn_W_out, L0_attn_skip, L0_attn_A_log, L0_attn_dt_bias)
    x = x + _L0_ffn_ref(_layernorm(x, axis=-1), L0_ffn_W1, L0_ffn_b1, L0_ffn_W2, L0_ffn_b2, L0_ffn_scale)
    return x

_drawn_inputs = setup_inputs


def setup_inputs(seed=0):
    import zlib

    import numpy as np

    out = dict(_drawn_inputs(seed))
    spreads = {'L0_attn_skip': (1.0, 0.2), 'L0_ffn_b1': (0.0, 0.352), 'L0_ffn_b2': (0.0, 0.1)}
    factors = {'L0_attn_dt_bias': 8.0}
    for name, (base, spread) in spreads.items():
        noise = np.random.default_rng([zlib.crc32(name.encode()), seed]).standard_normal(out[name].shape)
        drawn = base * np.exp(spread * noise) if base else spread * noise
        out[name] = jnp.asarray(drawn.astype(out[name].dtype))
    for name, factor in factors.items():
        out[name] = (out[name] * factor).astype(out[name].dtype)
    return out
```

```python
from contextlib import ExitStack

import numpy as np

import concourse.bass as bass
from concourse import mybir

F32 = mybir.dt.float32
ALU = mybir.AluOpType
ACT = mybir.ActivationFunctionType

P = 128
T = 2048
DM = 128
DI = 256
NH = 32
NS = 32
DH = DI // NH
KC = 4
FF = 512
L = 32
TB = 256
NB = T // TB
CH = TB // L
G = NH // 4
GC = G * CH
HG = GC // 2
TT = T // P
NQ = 4
U = G * TB
LN_EPS = 1e-5
NORM_EPS = 1e-8
DT_MIN, DT_MAX, K_MAX = 1e-4, 0.1, 0.5
FG = 4
FT = T // FG


def mixer_kernel(nc, a):
    with ExitStack() as ctx:
        def sb(name, shape):
            return ctx.enter_context(nc.sbuf_tensor(name, shape, F32))

        def sem(name):
            return ctx.enter_context(nc.semaphore(name))

        w_in = sb("w_in", [P, 2 * DI + 2 * NH])
        w_bc = sb("w_bc", [P, 2, NQ * NH * NS])
        w_out = sb("w_out", [P, 2, DM])
        conv_w = sb("conv_w", [P, 2, KC])
        conv_b = sb("conv_b", [P, 2])
        skip = sb("skip", [P, 2])
        dt_bias = sb("dt_bias", [P, NH])
        sel = sb("sel", [P, NH * NS])
        coef = sb("coef", [P, NH * NS])
        band = sb("band", [P, 60])
        ident = sb("ident", [P, P])
        causal = sb("causal", [P, L])
        one = sb("one", [P, 1])
        a_exp = sb("a_exp", [P, NS])
        ln_stats = sb("ln_stats", [P, TT, 6])
        ln_mv = sb("ln_mv", [P, TT, 2])
        ln_rstd = sb("ln_rstd", [P, TT])
        xnT = sb("xnT", [P, T])
        x1 = xnT[:, :].rearrange("p (i d) -> p i d", d=DM)
        x4 = sb("x4", [P, TB])
        xt = sb("xt", [P, 2, DM])
        raw = sb("raw", [P, NQ, GC, L])
        rt = sb("rt", [P, TB])
        pd = sb("pd", [P, GC, L + 1])
        pi = sb("pi", [P, GC, L + 1])
        bt = sb("bt", [P, GC, L + 1])
        alpha = sb("alpha", [P, GC, L])
        rec_t = sb("rec_t", [P, 2, 2, HG])
        Z = sb("Z", [P, 2, GC, L + 1])
        S = sb("S", [P, 2, GC, L + 1])
        E = sb("E", [P, 2, GC, L])
        C = sb("C", [P, 2, GC, L])
        psi_end = sb("psi_end", [P, 2, 2, G, CH])
        VR = sb("VR", [P, 2, TB + KC - 1])
        V = sb("V", [P, 2, TB])
        GS = sb("GS", [P, 2, TB])
        VT = sb("VT", [P, 2, CH, L])
        YG = sb("YG", [P, 2, TB])
        kin = sb("kin", [P, GC, 2, DH])
        st = sb("st", [P, 2, 2, G, DH])
        st_t = sb("st_t", [P, 2, G, DH])
        st_z = sb("st_z", [P, 2, G, DH])
        st_s = sb("st_s", [P, 2, G, DH])
        vb = sb("vb", [P, 2, 2, G, 4 * DH])
        GM = raw[:, 0]
        ub = raw[:, 1]
        ET = raw[:, 2:4]
        sq = C[:, 0].rearrange("p a b -> p (a b)").rearrange("p (k c) -> p k c", k=2)
        xT4 = raw[:, 0].rearrange("p a b -> p (a b)")
        xin = E[:, 0].rearrange("p a b -> p (a b)").rearrange("p (i d) -> p i d", d=DM)
        par = C[:, :].rearrange("p a b c -> p (a b c)")[:, 0:TT * 4 * NH].rearrange("p (i k h) -> p i k h", k=4, h=NH)
        tmpf = C[:, :].rearrange("p a b c -> p (a b c)")[:, 2048:4096].rearrange("p (k i h) -> p k i h", k=4, h=NH)
        wv = w_bc[:, :, :].rearrange("p a b -> p (a b)")
        w1 = wv[:, 0:FF]
        w2 = wv[:, FF:2 * FF].rearrange("p (b o) -> p b o", b=4)
        b2b = wv[:, 1024:1152]
        b1 = wv[:, 1152:1156]
        scale = wv[:, 1156:1157]
        lt = wv[:, 1280:1280 + 16 * DM]
        hT = wv[:, 4096:4096 + 2 * 4 * FT].rearrange("p (k b t) -> p k b t", k=2, b=4)
        xn2 = E[:, 0].rearrange("p a b -> p (a b)").rearrange("p (i d) -> p i d", d=DM)
        xn2T = E[:, 1].rearrange("p a b -> p (a b)")
        yout = C[:, 0].rearrange("p a b -> p (a b)").rearrange("p (i d) -> p i d", d=DM)

        ps = ctx.enter_context(nc.psum_tensor("ps", [P, 8, 512], F32))
        psf = ps[:, :, :].rearrange("p b c -> p (b c)")

        def slot(gh):
            return psf[:, 1024 * gh:1024 * gh + 1024]

        def slot3(gh):
            return slot(gh).rearrange("p (a l) -> p a l", l=L)

        w_loaded = sem("w_loaded")
        x_loaded = sem("x_loaded")
        xt_loaded = sem("xt_loaded")
        zeroed = sem("zeroed")
        pro = sem("pro")
        pro_act = sem("pro_act")
        pro_pe = sem("pro_pe")
        x4_stored = sem("x4_stored")
        x4_ready = sem("x4_ready")
        coef_mm = sem("coef_mm")
        d_out = sem("d_out")
        pd_ready = sem("pd_ready")
        ln_ready = sem("ln_ready")
        pi_ready = sem("pi_ready")
        newton = sem("newton")
        coef_used = sem("coef_used")
        rec_m = sem("rec_m")
        rec_a = sem("rec_a")
        val_mm = sem("val_mm")
        vr_ready = sem("vr_ready")
        gate_ready = sem("gate_ready")
        conv_step = sem("conv_step")
        tail_ready = sem("tail_ready")
        v_ready = sem("v_ready")
        vt_ready = sem("vt_ready")
        w_mm = sem("w_mm")
        sq_ready = sem("sq_ready")
        raw_ready = sem("raw_ready")
        nrm_mm = sem("nrm_mm")
        root = sem("root")
        rt_step = sem("rt_step")
        r_mm = sem("r_mm")
        normed = sem("normed")
        ec = sem("ec")
        et_ready = sem("et_ready")
        psi_ready = sem("psi_ready")
        ub_zero = sem("ub_zero")
        ub_ready = sem("ub_ready")
        begun = sem("begun")
        clearing = sem("clearing")
        g_mm = sem("g_mm")
        gm_ready = sem("gm_ready")
        k_mm = sem("k_mm")
        kin_ready = sem("kin_ready")
        st_step = sem("st_step")
        st_ready = sem("st_ready")
        vb_ready = sem("vb_ready")
        y_mm = sem("y_mm")
        yg_step = sem("yg_step")
        out_mm = sem("out_mm")
        x1_ready = sem("x1_ready")
        ffn_w = sem("ffn_w")
        lt_moved = sem("lt_moved")
        fv = sem("fv")
        fa = sem("fa")
        fp = sem("fp")
        h_mm = sem("h_mm")
        h_ready = sem("h_ready")
        o_mm = sem("o_mm")
        o_step = sem("o_step")
        stored = sem("stored")

        REC = 2 * 2 * L
        EC = 13
        PRO_XN = 2 * TT + 2 + 1
        PRO_EXP = 2 * TT + 2 + TT + 3
        PRO_PAR = PRO_EXP + 22
        PRO_ACT = 1 + 4 + 2 + 4
        FV_XN = 4 + TT
        block = ctx.enter_context(nc.Block())
        loads = [(w_in, a["w_in"]), (sel, a["sel"]), (band, a["band"]), (ident, a["ident"]),
                 (causal, a["causal"]), (conv_w, a["conv_w"]), (conv_b, a["conv_b"]), (skip, a["skip"]),
                 (w_out, a["w_out"])]
        NLOAD = len(loads) + 7

        @block.sync
        def _(sp):
            sp.dma_start(xin, a["x"].rearrange("(i p) d -> p i d", p=P)).then_inc(x_loaded, 16)
            for dst, src in loads:
                full = dst[:, :] if len(dst.shape) == 2 else dst[:, :, :]
                sp.dma_start(full, src).then_inc(w_loaded, 16)
            sp.dma_start(dt_bias[:, :], a["dt_bias"].partition_broadcast(P)).then_inc(w_loaded, 16)
            for r in range(0, P, NH):
                sp.dma_start(a_exp[r:r + 32, :], a["A_log"]).then_inc(w_loaded, 16)
            for half in range(2):
                sp.dma_start(w_bc[:, half, :], a["w_bc"][half]).then_inc(w_loaded, 16)
            xtiles = a["x"].rearrange("(b i p) d -> b p i d", i=2, p=P)

            x4_dram = a["x4"]
            sp.wait_ge(pro_act, PRO_ACT)
            sp.dma_start(x4_dram, xT4).then_inc(x4_stored, 16)
            sp.wait_ge(x4_stored, 16)
            x4_blocks = x4_dram.rearrange("p (b t) -> b p t", t=TB)

            def block_rows(b):
                sp.dma_start(x4[:, :], x4_blocks[b]).then_inc(x4_ready, 16)
                sp.wait_ge(x_loaded, 16)
                sp.wait_ge(x1_ready, b + 1)
                sp.dma_start(xt[:, :, :], xtiles[b]).then_inc(xt_loaded, 16)

            block_rows(0)
            with sp.Fori(1, NB) as b:
                sp.wait_ge(x4_stored, 16)
                sp.wait_ge(rt_step, 3 * b)
                block_rows(b)
            sp.wait_ge(w_mm, 8 * NB)
            sp.dma_start(w1, a["w1"]).then_inc(ffn_w, 16)
            sp.dma_start(w2, a["w2"]).then_inc(ffn_w, 16)
            sp.dma_start(b2b, a["b2"].partition_broadcast(P)).then_inc(ffn_w, 16)
            sp.dma_start(b1, a["b1"]).then_inc(ffn_w, 16)
            sp.dma_start(scale, a["scale"].partition_broadcast(P)).then_inc(ffn_w, 16)
            sp.wait_ge(fv, FV_XN)
            sp.dma_start(lt[0:1, :].rearrange("o (t d) -> o t d", d=DM), xn2[1:17, 0, :]).then_inc(lt_moved, 16)
            yd = a["y"].rearrange("(i p) d -> p i d", p=P)
            for f in range(FG):
                sp.wait_ge(o_step, 2 * (f + 1))
                sp.dma_start(yd[:, 4 * f:4 * f + 4, :], yout[:, 4 * f:4 * f + 4, :]).then_inc(stored, 16)
            sp.wait_ge(stored, 16 * FG)

        @block.tensor
        def _(pe):
            def coefficients(b):
                pe.wait_ge(x4_ready, 16 * b + 16)
                for kind, rows in enumerate((slice(64, 128), slice(32, 64), slice(0, 32))):
                    for gh in range(2):
                        if kind == 0:
                            pe.wait_ge(normed, 8 * b)
                        elif kind == 1:
                            pe.wait_ge(d_out, 2 * b + gh + 1)
                        else:
                            pe.wait_ge(coef_used, 4 * b + gh + 1)
                        for g4 in range(4):
                            g = 4 * gh + g4
                            mm = pe.matmul(slot(gh)[:, TB * g4:TB * g4 + TB], coef[rows, P * g:P * g + P],
                                           x4[rows, :], start=True, stop=True)
                        mm.then_inc(coef_mm, 1)

            def value_gate(b):
                pe.wait_ge(gm_ready, 4 * b)
                for k in range(2):
                    for half in range(2):
                        col = DI * k + P * half
                        mm = pe.matmul(ps[:, 6 + k, TB * half:TB * half + TB], w_in[:, col:col + P],
                                       xnT[:, bass.ts(b, TB)], start=True, stop=True)
                    mm.then_inc(val_mm, 1)

            def bc_products(b):
                def sums(k):
                    q, gh = k // 2, k % 2
                    pe.wait_ge(sq_ready, 8 * b + k + 1)
                    for g4 in range(4):
                        g = 4 * gh + g4
                        mm = pe.matmul(ps[32 * q:32 * q + 32, 4, 0:TB], band[:, 28 - 4 * g:60 - 4 * g],
                                       sq[:, k % 2, TB * g4:TB * g4 + TB], start=(g == 0), stop=(g == G - 1))
                    mm.then_inc(nrm_mm, 1)

                pe.wait_ge(v_ready, 2 * b + 2)
                pe.wait_ge(kin_ready, 4 * b)
                pe.wait_ge(coef_used, 4 * b + 4)
                pe.wait_ge(yg_step, 3 * b)
                for k in range(8):
                    q, gh = k // 2, k % 2
                    if k >= 2:
                        pe.wait_ge(raw_ready, 8 * b + k - 1)
                    for g4 in range(4):
                        col = (q * G + 4 * gh + g4) * P
                        for half in range(2):
                            mm = pe.matmul(slot(gh)[:, TB * g4:TB * g4 + TB], w_bc[:, half, col:col + P],
                                           V[:, half, :], start=(half == 0), stop=(half == 1))
                    mm.then_inc(w_mm, 1)
                    if k >= 1:
                        sums(k - 1)
                sums(7)

            def scales(b):
                pe.wait_ge(rt_step, 3 * b + 3)
                pe.wait_ge(raw_ready, 8 * b + 8)
                for k in range(8):
                    q, gh = k // 2, k % 2
                    if k >= 2:
                        pe.wait_ge(normed, 8 * b + k - 1)
                    for g4 in range(4):
                        g = 4 * gh + g4
                        mm = pe.matmul(slot(gh)[:, TB * g4:TB * g4 + TB], sel[32 * q:32 * q + 32, P * g:P * g + P],
                                       rt[32 * q:32 * q + 32, :], start=True, stop=True)
                    mm.then_inc(r_mm, 1)

            def scores(b):
                pe.wait_ge(ec, EC * b + EC)
                pe.wait_ge(root, b + 1)
                pe.wait_ge(x1_ready, b + 1)
                pe.wait_ge(vr_ready, b + 1)
                pe.wait_ge(gate_ready, b + 1)
                pe.sem_inc(begun, 1)
                for m in range(GC // 4):
                    for r in range(4):
                        for comp in range(2):
                            for j in range(4):
                                bank = (j + r) % 4
                                gc = (GC // 4) * bank + m
                                rows = slice(32 * j, 32 * j + 32)
                                mm = pe.matmul(ps[rows, 4 + bank, L * m:L * m + L], E[rows, comp, gc, :],
                                               C[rows, comp, gc, :], start=(comp == 0), stop=(comp == 1))
                mm.then_inc(g_mm, 1)

            def chunk_inputs(b, last):
                if last:
                    pe.wait_ge(normed, 8 * b + 8)
                else:
                    pe.wait_ge(coef_used, 4 * b + 8)
                pe.wait_ge(et_ready, 2 * b + 2)
                pe.wait_ge(ub_ready, 16 * b + 16)
                pe.sem_inc(begun, 1)
                for m in range(GC // 4):
                    for r in range(4):
                        for comp in range(2):
                            for j in range(4):
                                bank = (j + r) % 4
                                gc = (GC // 4) * bank + m
                                rows = slice(32 * j, 32 * j + 32)
                                col = 2 * DH * m + DH * comp
                                mm = pe.matmul(ps[rows, bank, col:col + DH], ET[rows, comp, gc, :],
                                               ub[rows, gc, DH * j:DH * j + DH], start=True, stop=True)
                mm.then_inc(k_mm, 1)

            def outputs(b):
                pe.wait_ge(gm_ready, 4 * b + 4)
                for c in range(CH):
                    pe.wait_ge(vb_ready, 32 * b + 4 * c + 5)
                    for g in range(G):
                        gc = g * CH + c
                        out = ps[32 * (g % 4):32 * (g % 4) + 32, 4, (g // 4) * TB + c * L:(g // 4) * TB + c * L + L]
                        pe.matmul(out, ub[:, gc, :], GM[:, gc, :], start=True, stop=False)
                        pe.matmul(out, vb[:, c % 2, 0, g, :], C[:, 0, gc, :], start=False, stop=False)
                        mm = pe.matmul(out, vb[:, c % 2, 1, g, :], C[:, 1, gc, :], start=False, stop=True)
                    mm.then_inc(y_mm, 1)
                pe.wait_ge(yg_step, 3 * b + 3)
                for i in range(2):
                    for half in range(2):
                        mm = pe.matmul(ps[:, 5, DM * i:DM * i + DM], YG[:, half, P * i:P * i + P], w_out[:, half, :],
                                       start=(half == 0), stop=(half == 1))
                mm.then_inc(out_mm, 1)

            pe.wait_ge(w_loaded, 16 * NLOAD)
            for i in range(TT):
                pe.wait_ge(pro, PRO_XN + i)
                pe.transpose(psf[:, DM * i:DM * i + DM], xin[:, i, :], ident[:, :]).then_inc(pro_pe, 1)
            for i in range(TT):
                pe.wait_ge(pro_act, 1 + i // 4 + 1)
                mm = pe.matmul(psf[:, 2048 + 64 * i:2048 + 64 * i + 64], xnT[:, P * i:P * i + P],
                               w_in[:, 2 * DI:], start=True, stop=True)
            mm.then_inc(pro_pe, 1)
            pe.wait_ge(pro, PRO_PAR)
            for i in range(TT):
                mm = pe.transpose(psf[:, P * i:P * i + P], par[:, i].rearrange("p k h -> p (k h)"), ident[:, :])
            mm.then_inc(pro_pe, 1)
            pe.wait_ge(pro_act, PRO_ACT)

            coefficients(0)
            value_gate(0)
            bc_products(0)
            scales(0)
            with pe.Fori(1, NB) as b:
                coefficients(b)
                scores(b - 1)
                chunk_inputs(b - 1, False)
                outputs(b - 1)
                value_gate(b)
                bc_products(b)
                scales(b)
            scores(NB - 1)
            chunk_inputs(NB - 1, True)
            outputs(NB - 1)

            for i in range(TT):
                pe.wait_ge(fv, 4 + i + 1)
                pe.transpose(psf[:, DM * i:DM * i + DM], xn2[:, i, :], ident[:, :]).then_inc(fp, 1)
            pe.wait_ge(lt_moved, 16)
            pe.wait_ge(x1_ready, NB + 1)

            def token(t, lo=0, n=DM, step=1):
                return lt[0:1, (t - 1) * DM + lo:(t - 1) * DM + lo + (n - 1) * step + 1:step]
            for r in range(4):
                pe.matmul(ps[:, 4, DM * r:DM * r + DM], token(2 + 2 * r), token(1 + 2 * r), start=True, stop=True)
            for q in range(4):
                for r in range(4):
                    mm = pe.matmul(ps[:, 5, DM * q + 32 * r:DM * q + 32 * r + 32], token(10 + 2 * r),
                                   token(9 + 2 * r, q, 32, 4), start=True, stop=True)
            mm.then_inc(fp, 1)

            def hidden(f):
                for hb in range(4):
                    pe.wait_ge(fa, f + 2)
                    pe.wait_ge(fv, FV_XN + 3)
                    k = 4 * f + hb
                    if k >= 2:
                        pe.wait_ge(h_ready, k - 1)
                    pe.matmul(ps[:, 6 + k % 2, :], w1[:, P * hb:P * hb + P], xn2T[:, FT * f:FT * f + FT],
                              start=True, stop=True).then_inc(h_mm, 1)

            def back(f):
                pe.wait_ge(h_ready, 4 * f + 4)
                if f >= 2:
                    pe.wait_ge(o_step, 2 * f - 3)
                for i in range(4):
                    for hb in range(4):
                        mm = pe.matmul(ps[:, 4 + f % 2, DM * i:DM * i + DM], hT[:, f % 2, hb, P * i:P * i + P],
                                       w2[:, hb, :], start=(hb == 0), stop=(hb == 3))
                mm.then_inc(o_mm, 1)

            hidden(0)
            for f in range(FG):
                if f + 1 < FG:
                    hidden(f + 1)
                back(f)

        @block.scalar
        def _(act):
            def coefficients(b):
                for gh in range(2):
                    act.wait_ge(coef_mm, 6 * b + gh + 1)
                    if gh == 0:
                        act.wait_ge(rec_a, REC * b)
                    act.activation(bt[:, HG * gh:HG * gh + HG, 1:], slot3(gh), ACT.Copy).then_inc(d_out, 1)
                act.wait_ge(pd_ready, b + 1)
                act.activation(bt[:, :, 1:], pd[:, :, 1:], ACT.Ln).then_inc(ln_ready, 1)
                act.wait_ge(ln_ready, b + 1)
                act.activation(pi[:, :, 1:], bt[:, :, 1:], ACT.Exp, scale=-1.0).then_inc(pi_ready, 1)

            def front(b):
                act.wait_ge(val_mm, 2 * b + 1)
                act.wait_ge(tail_ready, b + 1)
                act.activation(VR[:, :, KC - 1:], ps[:, 6, :].rearrange("p (h t) -> p h t", h=2),
                               ACT.Copy).then_inc(vr_ready, 1)
                act.wait_ge(val_mm, 2 * b + 2)
                act.wait_ge(yg_step, 3 * b)
                act.activation(GS[:, :, :], ps[:, 7, :].rearrange("p (h t) -> p h t", h=2),
                               ACT.Silu).then_inc(gate_ready, 1)
                act.wait_ge(conv_step, 8 * b + 8)
                for half in range(2):
                    act.activation(V[:, half, :], YG[:, half, :], ACT.Silu,
                                   bias=conv_b[:, half:half + 1]).then_inc(v_ready, 1)
                for k in range(8):
                    q, gh = k // 2, k % 2
                    act.wait_ge(w_mm, 8 * b + k + 1)
                    if k >= 2:
                        act.wait_ge(nrm_mm, 8 * b + k - 1)
                    act.activation(sq[:, k % 2, :], slot(gh), ACT.Square).then_inc(sq_ready, 1)
                    act.activation(raw[:, q, HG * gh:HG * gh + HG, :], slot3(gh), ACT.Copy).then_inc(raw_ready, 1)
                act.wait_ge(nrm_mm, 8 * b + 8)
                act.activation(rt[:, :], ps[:, 4, 0:TB], ACT.Sqrt).then_inc(root, 1)

            def values(b):
                act.wait_ge(ub_zero, b + 1)
                act.wait_ge(vt_ready, b + 1)
                ubv = ub.rearrange("p (e f c) m -> p e f c m", e=2, f=4)
                for j in range(4):
                    for g4 in range(4):
                        act.activation(ubv[32 * j:32 * j + 32, :, g4, :, DH * j:DH * j + DH],
                                       VT[32 * g4:32 * g4 + 32, :, :, DH * j:DH * j + DH],
                                       ACT.Copy).then_inc(ub_ready, 1)

            def back(b):
                act.wait_ge(k_mm, b + 1)
                for i in range(4):
                    act.activation(kin[:, 16 * i:16 * i + 16].rearrange("p a c d -> p (a c d)"), ps[:, i, 0:256],
                                   ACT.Copy).then_inc(kin_ready, 1)
                for c in range(CH):
                    act.wait_ge(st_ready, 16 * b + 2 * c + 1)
                    if c >= 2:
                        act.wait_ge(y_mm, 8 * b + c - 1)
                    for j in range(4):
                        rows = slice(32 * j, 32 * j + 32)
                        act.activation(vb[rows, c % 2, :, :, DH * j:DH * j + DH], st[rows, c % 2],
                                       ACT.Copy).then_inc(vb_ready, 1)

            act.wait_ge(pro, 2 * TT + 1)
            act.activation(ln_rstd[:, :], ln_mv[:, :, 1], ACT.Sqrt).then_inc(pro_act, 1)
            for k in range(4):
                act.wait_ge(pro_pe, 4 * k + 4)
                act.activation(xnT[:, 512 * k:512 * k + 512], ps[:, k, :], ACT.Copy).then_inc(pro_act, 1)
            act.wait_ge(w_loaded, 16 * NLOAD)
            act.wait_ge(pro, PRO_EXP)
            act.activation(tmpf[:, 0:2], tmpf[:, 2:4], ACT.Exp).then_inc(pro_act, 1)
            act.activation(a_exp[:, :], a_exp[:, :], ACT.Exp).then_inc(pro_act, 1)
            act.wait_ge(pro_pe, TT + 2)
            for k in range(4):
                act.activation(xT4[:, 512 * k:512 * k + 512], ps[:, k, :], ACT.Copy).then_inc(pro_act, 1)
            coefficients(0)
            front(0)
            values(0)
            with act.Fori(1, NB) as b:
                coefficients(b)
                back(b - 1)
                front(b)
                values(b)
            back(NB - 1)

            act.wait_ge(fv, 2)
            act.activation(ln_rstd[:, :], ln_mv[:, :, 1], ACT.Sqrt).then_inc(fa, 1)
            for k in range(FG):
                act.wait_ge(fp, 4 * k + 4)
                act.activation(xn2T[:, 512 * k:512 * k + 512], ps[:, k, :], ACT.Copy).then_inc(fa, 1)
            for k in range(4 * FG):
                f, hb = k // 4, k % 4
                act.wait_ge(h_mm, k + 1)
                if hb == 0 and f >= 2:
                    act.wait_ge(o_mm, f - 1)
                act.activation(hT[:, f % 2, hb, :], ps[:, 6 + k % 2, :], ACT.Gelu,
                               bias=b1[:, hb:hb + 1]).then_inc(h_ready, 1)

        @block.gpsimd
        def _(pool):
            def clear_values(b):
                pool.wait_ge(ec, EC * b + EC)
                pool.sem_inc(clearing, 1)
                pool.memset(ub, 0.0).then_inc(ub_zero, 1)

            def states(b):
                pool.wait_ge(kin_ready, 4 * b + 4)
                pool.wait_ge(psi_ready, 2 * b + 2)
                kv = kin[:, :].rearrange("p (g c) k d -> p c k g d", c=CH)
                for c in range(CH):
                    pool.wait_ge(st_ready, 16 * b + 2 * c + 1)
                    pool.tensor_tensor(st_t[:, :], st[:, c % 2], kv[:, c], ALU.add).then_inc(st_step, 1)
                    pool.wait_ge(st_step, 24 * b + 3 * c + 1)
                    for i, dst in enumerate((st_z, st_s)):
                        m = psi_end[:, i, :, :, c].unsqueeze(3).broadcast_to([P, 2, G, DH])
                        pool.tensor_tensor(dst[:, :], st_t[:, :], m, ALU.mult).then_inc(st_step, 1)
                    pool.wait_ge(vb_ready, 32 * b + 4 * c + 1)
                    for i, src in enumerate((st_z, st_s)):
                        pool.wait_ge(st_step, 24 * b + 3 * c + 2 + i)
                        pool.tensor_tensor(st[:, (c + 1) % 2, i], src[:, 0], src[:, 1], ALU.add).then_inc(st_ready, 1)

            pool.memset(bt[:, :, 0:1], 0.0).then_inc(zeroed, 1)
            pool.memset(VR[:, :, 0:KC - 1], 0.0).then_inc(zeroed, 1)
            pool.memset(st[:, :], 0.0).then_inc(st_ready, 1)
            pool.memset(vb[:, :], 0.0).then_inc(vb_ready, 1)
            pool.memset(Z[:, 0, :, 0:1], 1.0).then_inc(zeroed, 1)
            pool.memset(Z[:, 1, :, 0:1], 0.0).then_inc(zeroed, 1)
            pool.memset(S[:, 0, :, 0:1], 0.0).then_inc(zeroed, 1)
            pool.memset(S[:, 1, :, 0:1], 1.0).then_inc(zeroed, 1)
            pool.memset(one[:, :], 1.0).then_inc(zeroed, 1)
            pool.wait_ge(zeroed, 7)
            pool.wait_ge(pro_act, PRO_ACT)
            clear_values(0)
            with pool.Fori(1, NB) as b:
                states(b - 1)
                clear_values(b)
            states(NB - 1)

        @block.vector
        def _(dve):
            def coefficients(b):
                dve.wait_ge(d_out, 2 * b + 2)
                dve.wait_ge(ec, EC * b)
                dve.tensor_tensor_scan(pd[:, :, :].rearrange("p a l -> p (a l)"), bt[:, :, :].rearrange("p a l -> p (a l)"),
                                       one[:, 0:1].broadcast_to([P, GC * (L + 1)]), 1.0, ALU.mult, ALU.max
                                       ).then_inc(pd_ready, 1)
                dve.wait_ge(pi_ready, b + 1)
                dve.tensor_tensor(bt[:, :, 1:], pd[:, :, 1:], pi[:, :, 1:], ALU.mult).then_inc(newton, 1)
                for gh in range(2):
                    r = slice(HG * gh, HG * gh + HG)
                    dve.wait_ge(coef_mm, 6 * b + 3 + gh)
                    dve.tensor_tensor(alpha[:, r], slot3(gh), pd[:, r, 0:L], ALU.mult).then_inc(coef_used, 1)
                dve.wait_ge(newton, 2 * b + 1)
                dve.scalar_tensor_tensor(out=pi[:, :, 1:], in0=bt[:, :, 1:], scalar=2.0, in1=pi[:, :, 1:],
                                         op0=ALU.subtract, op1=ALU.mult, reverse0=True).then_inc(newton, 1)
                dve.wait_ge(newton, 2 * b + 2)
                for gh in range(2):
                    r = slice(HG * gh, HG * gh + HG)
                    dve.wait_ge(coef_mm, 6 * b + 5 + gh)
                    dve.tensor_tensor(bt[:, r, 1:], slot3(gh), pi[:, r, 1:], ALU.mult).then_inc(coef_used, 1)

            def recursion(b):
                dve.wait_ge(coef_used, 4 * b + 4)
                for k in range(L):
                    for i, (coefs, src, dst) in enumerate(((alpha[:, :, k], S[:, :, :, k], Z),
                                                           (bt[:, :, k + 1], Z[:, :, :, k + 1], S))):
                        n = 4 * k + 2 * i
                        for gh in range(2):
                            r = slice(HG * gh, HG * gh + HG)
                            if n:
                                dve.wait_ge(rec_a, REC * b + n - 2 + gh + 1)
                            m = coefs[:, r].unsqueeze(1).broadcast_to([P, 2, HG])
                            dve.tensor_tensor(rec_t[:, gh], m, src[:, :, r], ALU.mult).then_inc(rec_m, 1)
                        for gh in range(2):
                            r = slice(HG * gh, HG * gh + HG)
                            dve.wait_ge(rec_m, REC * b + n + gh + 1)
                            dve.tensor_tensor(dst[:, :, r, k + 1], dst[:, :, r, k], rec_t[:, gh],
                                              ALU.add if i else ALU.subtract).then_inc(rec_a, 1)

            def convolution(b):
                dve.wait_ge(vr_ready, b + 1)
                for half in range(2):
                    dve.tensor_scalar(YG[:, half, :], VR[:, half, 0:TB], conv_w[:, half, 0:1], None,
                                      ALU.mult).then_inc(conv_step, 1)
                for k in range(1, KC):
                    for half in range(2):
                        dve.wait_ge(conv_step, 8 * b + 2 * (k - 1) + half + 1)
                        dve.scalar_tensor_tensor(out=YG[:, half, :], in0=VR[:, half, k:k + TB],
                                                 scalar=conv_w[:, half, k:k + 1], in1=YG[:, half, :],
                                                 op0=ALU.mult, op1=ALU.add).then_inc(conv_step, 1)
                dve.wait_ge(conv_step, 8 * b + 8)
                dve.tensor_copy(VR[:, :, 0:KC - 1], VR[:, :, TB:]).then_inc(tail_ready, 1)
                dve.wait_ge(v_ready, 2 * b + 2)
                dve.transpose(VT[:, :].rearrange("p a b c -> p (a b c)"),
                              V[:, :, :].rearrange("p a b -> p (a b)")).then_inc(vt_ready, 1)

            def row_scales(b):
                dve.wait_ge(root, b + 1)
                dve.wait_ge(x4_ready, 16 * b + 16)
                dve.tensor_scalar(rt[:, :], rt[:, :], NORM_EPS, None, ALU.add).then_inc(rt_step, 1)
                dve.wait_ge(rt_step, 3 * b + 1)
                dve.reciprocal(rt[:, :], rt[:, :]).then_inc(rt_step, 1)
                dve.wait_ge(rt_step, 3 * b + 2)
                dve.tensor_tensor(rt[0:64, :], rt[0:64, :], x4[0:64, :], ALU.mult).then_inc(rt_step, 1)

            def chunk_operands(b):
                for k in range(8):
                    q, gh = k // 2, k % 2
                    r = slice(HG * gh, HG * gh + HG)
                    dve.wait_ge(r_mm, 8 * b + k + 1)
                    dve.tensor_tensor(raw[:, q, r], raw[:, q, r], slot3(gh), ALU.mult).then_inc(normed, 1)
                def step(out, x, y, op, after=0):
                    dve.wait_ge(ec, EC * b + after)
                    dve.tensor_tensor(out, x, y, op).then_inc(ec, 1)
                dve.wait_ge(normed, 8 * b + 8)
                dve.wait_ge(rec_a, REC * b + REC)
                bz, bx, cz, cx = (raw[:, q] for q in range(4))
                step(bz, bz, pd[:, :, 0:L], ALU.mult)
                step(cz, cz, pi[:, :, 1:], ALU.mult)
                step(C[:, 0], bx, Z[:, 0, :, 1:], ALU.mult)
                step(E[:, 0], bz, S[:, 1, :, 0:L], ALU.mult, 1)
                step(E[:, 1], bz, S[:, 0, :, 0:L], ALU.mult, 1)
                step(C[:, 1], bx, Z[:, 1, :, 1:], ALU.mult)
                step(E[:, 1], C[:, 0], E[:, 1], ALU.subtract, 5)
                step(E[:, 0], E[:, 0], C[:, 1], ALU.subtract, 6)
                step(raw[:, 0], cx, S[:, 0, :, 1:], ALU.mult, 5)
                step(C[:, 0], cz, Z[:, 0, :, 1:], ALU.mult, 7)
                step(C[:, 1], cz, Z[:, 1, :, 1:], ALU.mult, 8)
                step(raw[:, 1], cx, S[:, 1, :, 1:], ALU.mult, 6)
                dve.wait_ge(ec, EC * b + 12)
                dve.tensor_tensor(C[:, :].rearrange("p k a l -> p (k a l)"), C[:, :].rearrange("p k a l -> p (k a l)"),
                                  raw[:, 0:2].rearrange("p k a l -> p (k a l)"), ALU.add).then_inc(ec, 1)
                for comp in range(2):
                    dve.transpose(ET[:, comp].rearrange("p a l -> p (a l)"),
                                  E[:, comp].rearrange("p a l -> p (a l)")).then_inc(et_ready, 1)
                dve.wait_ge(st_ready, 16 * b + 1)
                pe2 = psi_end[:, :].rearrange("p i k g c -> p i k (g c)")
                dve.tensor_tensor(pe2[:, 0], Z[:, :, :, L], pi[:, :, L].unsqueeze(1).broadcast_to([P, 2, GC]),
                                  ALU.mult).then_inc(psi_ready, 1)
                dve.tensor_copy(pe2[:, 1], S[:, :, :, L]).then_inc(psi_ready, 1)

            def mask_scores(b):
                dve.wait_ge(g_mm, b + 1)
                for i in range(4):
                    dve.tensor_tensor(GM[:, 16 * i:16 * i + 16, :], ps[:, 4 + i, :].rearrange("p (a l) -> p a l", l=L),
                                      causal[:, :].unsqueeze(1).broadcast_to([P, 16, L]), ALU.mult).then_inc(gm_ready, 1)

            def gated(b):
                dve.wait_ge(y_mm, 8 * b + 8)
                for half in range(2):
                    dve.scalar_tensor_tensor(out=YG[:, half, :], in0=V[:, half, :], scalar=skip[:, half:half + 1],
                                             in1=ps[:, 4, TB * half:TB * half + TB], op0=ALU.mult,
                                             op1=ALU.add).then_inc(yg_step, 1)
                dve.wait_ge(yg_step, 3 * b + 2)
                dve.tensor_tensor(YG[:, :, :], YG[:, :, :], GS[:, :, :], ALU.mult).then_inc(yg_step, 1)
                dve.wait_ge(out_mm, b + 1)
                dve.wait_ge(xt_loaded, 16 * b + 16)
                dve.tensor_tensor(xnT[:, bass.ts(b, TB)], ps[:, 5, 0:TB], xt[:, :, :].rearrange("p i d -> p (i d)"),
                                  ALU.add).then_inc(x1_ready, 1)

            count = [0]

            def link(ins):
                count[0] += 1
                ins.then_inc(pro, 1)
                dve.wait_ge(pro, count[0])

            dve.wait_ge(x_loaded, 16)
            for i in range(TT):
                dve.bn_stats(ln_stats[:, i, :], xin[:, i, :]).then_inc(pro, 1)
            for i in range(TT):
                dve.wait_ge(pro, i + 1)
                dve.bn_aggr(ln_mv[:, i, :], ln_stats[:, i, :]).then_inc(pro, 1)
            count[0] = 2 * TT
            dve.wait_ge(pro, 2 * TT)
            link(dve.tensor_scalar(ln_mv[:, :, 1], ln_mv[:, :, 1], LN_EPS, None, ALU.add))
            dve.wait_ge(pro_act, 1)
            link(dve.reciprocal(ln_rstd[:, :], ln_rstd[:, :]))
            for i in range(TT):
                dve.tensor_scalar(xin[:, i, :], xin[:, i, :], ln_mv[:, i, 0:1], ln_rstd[:, i:i + 1],
                                  ALU.subtract, ALU.mult).then_inc(pro, 1)
            count[0] += TT
            dve.wait_ge(w_loaded, 16 * NLOAD)
            dve.wait_ge(pro, count[0])
            dve.wait_ge(pro_pe, TT + 1)
            pp = psf[:, 2048:3072].rearrange("p (i k h) -> p i k h", k=2, h=NH)
            dtb = dt_bias[:, :].unsqueeze(1).broadcast_to([P, TT, NH])
            link(dve.tensor_tensor(tmpf[:, 2], pp[:, :, 0], dtb, ALU.add))
            link(dve.tensor_scalar(tmpf[:, 2], tmpf[:, 2], 0.0, None, ALU.min))
            link(dve.tensor_scalar(tmpf[:, 3], pp[:, :, 1], -1.0, None, ALU.mult))
            assert count[0] == PRO_EXP
            dve.wait_ge(pro_act, 1 + 4 + 1)
            v, w, t2, t3 = (tmpf[:, k] for k in range(4))
            dt, dt_again, dt2, cc = (par[:, :, k] for k in range(4))
            link(dve.tensor_scalar(v, v, 0.11, None, ALU.min))
            link(dve.tensor_scalar(t2, v, 2.0, None, ALU.add))
            link(dve.reciprocal(t2, t2))
            link(dve.tensor_tensor(v, v, t2, ALU.mult))
            link(dve.tensor_tensor(t2, v, v, ALU.mult))
            link(dve.tensor_scalar(t3, t2, 2.0 / 7, 2.0 / 5, ALU.mult, ALU.add))
            link(dve.tensor_tensor(t3, t3, t2, ALU.mult))
            link(dve.tensor_scalar(t3, t3, 2.0 / 3, None, ALU.add))
            link(dve.tensor_tensor(t3, t3, t2, ALU.mult))
            link(dve.tensor_scalar(t3, t3, 2.0, None, ALU.add))
            link(dve.tensor_tensor(t3, t3, v, ALU.mult))
            link(dve.tensor_scalar(dt, t3, DT_MIN, DT_MAX, ALU.max, ALU.min))
            link(dve.tensor_copy(dt_again, dt))
            link(dve.tensor_tensor(dt2, dt, dt, ALU.mult))
            link(dve.tensor_scalar(w, w, 1.0, None, ALU.add))
            link(dve.reciprocal(w, w))
            link(dve.tensor_tensor(w, w, dt, ALU.mult))
            link(dve.tensor_scalar(cc, w, K_MAX, 1.0, ALU.mult, ALU.add))
            dve.wait_ge(pro_act, 1 + 4 + 2)
            link(dve.tensor_copy(coef[0:32, :], sel[0:32, :]))
            link(dve.tensor_copy(coef[96:128, :], sel[96:128, :]))
            for r in (32, 64):
                rows = slice(r, r + 32)
                link(dve.tensor_tensor(coef[rows, :].rearrange("p (h n) -> p h n", n=NS),
                                       sel[rows, :].rearrange("p (h n) -> p h n", n=NS),
                                       a_exp[rows, :].unsqueeze(1).broadcast_to([32, NH, NS]), ALU.mult))
            assert count[0] == PRO_PAR, (count[0], PRO_PAR)
            dve.wait_ge(zeroed, 7)
            dve.tensor_copy(VR[:, :, 0:KC - 1], VR[:, :, 0:KC - 1]).then_inc(tail_ready, 1)
            dve.sem_inc(x1_ready, 1)

            coefficients(0)
            recursion(0)
            convolution(0)
            row_scales(0)
            chunk_operands(0)
            with dve.Fori(1, NB) as b:
                coefficients(b)
                mask_scores(b - 1)
                recursion(b)
                gated(b - 1)
                convolution(b)
                row_scales(b)
                chunk_operands(b)
            mask_scores(NB - 1)
            gated(NB - 1)

            dve.wait_ge(x1_ready, NB + 1)
            for i in range(TT):
                ins = dve.bn_stats(ln_stats[:, i, :], x1[:, i, :])
                ins.then_inc(pro, 1)
            for i in range(TT):
                dve.wait_ge(pro, PRO_PAR + i + 1)
                dve.bn_aggr(ln_mv[:, i, :], ln_stats[:, i, :]).then_inc(pro, 1)
            dve.wait_ge(pro, PRO_PAR + 2 * TT)
            dve.tensor_scalar(ln_mv[:, :, 1], ln_mv[:, :, 1], LN_EPS, None, ALU.add).then_inc(fv, 2)
            dve.wait_ge(fa, 1)
            dve.reciprocal(ln_rstd[:, :], ln_rstd[:, :]).then_inc(fv, 2)
            dve.wait_ge(fv, 4)
            for i in range(TT):
                dve.tensor_scalar(xn2[:, i, :], x1[:, i, :], ln_mv[:, i, 0:1], ln_rstd[:, i:i + 1],
                                  ALU.subtract, ALU.mult).then_inc(fv, 1)
            dve.wait_ge(ffn_w, 16 * 5)
            dve.wait_ge(fp, TT + 1)
            dve.scalar_tensor_tensor(out=w1, in0=ps[:, 4, :], scalar=scale, in1=w1, op0=ALU.mult,
                                     op1=ALU.add).then_inc(fv, 1)
            dve.scalar_tensor_tensor(out=w2, in0=ps[:, 5, :].rearrange("p (b o) -> p b o", b=4), scalar=scale,
                                     in1=w2, op0=ALU.mult, op1=ALU.add).then_inc(fv, 1)
            dve.tensor_tensor(x1, x1, b2b.unsqueeze(1).broadcast_to([P, TT, DM]), ALU.add).then_inc(fv, 1)
            dve.wait_ge(fv, FV_XN + 3)
            for f in range(FG):
                dve.wait_ge(o_mm, f + 1)
                dve.tensor_tensor(yout[:, 4 * f:4 * f + 4, :], ps[:, 4 + f % 2, :].rearrange("p (i d) -> p i d", d=DM),
                                  x1[:, 4 * f:4 * f + 4, :], ALU.add).then_inc(o_step, 2)


_SHAPES = {"x": (T, DM), "w_in": (DM, 2 * DI + 2 * NH), "w_bc": (2, P, NQ * NH * NS), "w_out": (P, 2, DM),
           "conv_w": (P, 2, KC), "conv_b": (P, 2), "skip": (P, 2), "dt_bias": (NH,), "A_log": (NH, NS),
           "w1": (DM, FF), "w2": (P, 4, DM), "b1": (P, 4), "b2": (DM,), "scale": (1,),
           "sel": (P, NH * NS), "band": (P, 60), "ident": (P, P), "causal": (P, L)}


def kernel(**inputs):
    import numpy as _np
    import concourse.bacc as _bacc
    from concourse.bass_utils import run_bass_kernel_spmd as _run

    f = {k: _np.asarray(v) for k, v in inputs.items()}
    win = f["L0_attn_W_in"]
    win = _np.concatenate([win[DI:2 * DI], win[:DI], win[2 * DI::2], win[2 * DI + 1::2]], axis=0).T
    wbc = f["L0_attn_W_bc"].reshape(G, 4, NQ, NS, 2, P).transpose(4, 5, 2, 0, 1, 3).reshape(2, P, NQ * NH * NS)

    def halves(v):
        return v.reshape((2, P) + v.shape[1:]).swapaxes(0, 1)
    rows = _np.arange(P)
    cols = _np.arange(NH * NS)
    arrays = {
        "x": f["L0_attn_x"].reshape(T, DM), "w_in": win, "w_bc": wbc,
        "w_out": f["L0_attn_W_out"].T.reshape(2, P, DM).swapaxes(0, 1),
        "conv_w": halves(f["L0_attn_dw_weight"]), "conv_b": halves(f["L0_attn_dw_bias"]),
        "skip": halves(f["L0_attn_skip"]), "dt_bias": f["L0_attn_dt_bias"], "A_log": f["L0_attn_A_log"],
        "w1": f["L0_ffn_W1"].T, "w2": f["L0_ffn_W2"].T.reshape(4, P, DM).swapaxes(0, 1),
        "b1": f["L0_ffn_b1"].reshape(4, P).T, "b2": f["L0_ffn_b2"], "scale": f["L0_ffn_scale"].reshape(1),
        "sel": (rows[:, None] % NH == cols[None, :] // NS).astype(_np.float32),
        "band": (_np.arange(60)[None, :] == 28 + rows[:, None] // NS).astype(_np.float32),
        "ident": _np.eye(P, dtype=_np.float32),
        "causal": (rows[:, None] % L <= _np.arange(L)[None, :]).astype(_np.float32),
    }
    nc = _bacc.Bacc("TRN2", target_bir_lowering=False, num_devices=1)
    args, feed = {}, {}
    for name, shape in _SHAPES.items():
        arr = _np.ascontiguousarray(arrays[name])
        assert arr.shape == shape, (name, arr.shape, shape)
        feed[f"in_{name}"] = arr
        args[name] = nc.dram_tensor(f"in_{name}", shape, F32, kind="ExternalInput").ap()
    args["x4"] = nc.dram_tensor("x4_scratch", (P, T), F32, kind="Internal").ap()
    args["y"] = nc.dram_tensor("out_y", (T, DM), F32, kind="ExternalOutput").ap()
    mixer_kernel(nc, args)
    r = _run(nc, [feed], core_ids=[0])
    return r.results[0]["out_y"].reshape(1, T, DM)
```

```python
from contextlib import ExitStack

import numpy as np

import concourse.bass as bass
from concourse import mybir

F32 = mybir.dt.float32
BF16 = mybir.dt.bfloat16
ALU = mybir.AluOpType
ACT = mybir.ActivationFunctionType

P = 128
T = 2048
DM = 128
DI = 256
NH = 32
NS = 32
DH = DI // NH
KC = 4
FF = 512
L = 32
TB = 256
NB = T // TB
CH = TB // L
G = NH // 4
GC = G * CH
HG = GC // 2
TT = T // P
NQ = 4
U = G * TB
LN_EPS = 1e-5
NORM_EPS = 1e-8
DT_MIN, DT_MAX, K_MAX = 1e-4, 0.1, 0.5
FG = 4
FT = T // FG


def mixer_kernel(nc, a):
    with ExitStack() as ctx:
        def sb(name, shape, dt=F32):
            return ctx.enter_context(nc.sbuf_tensor(name, shape, dt))

        def sem(name):
            return ctx.enter_context(nc.semaphore(name))

        w_in = sb("w_in", [P, 2 * DI + 2 * NH])
        w_bc = sb("w_bc", [P, 2, NQ * NH * NS])
        w_out = sb("w_out", [P, 2, DM])
        conv_w = sb("conv_w", [P, 2, KC])
        conv_b = sb("conv_b", [P, 2])
        skip = sb("skip", [P, 2])
        dt_bias = sb("dt_bias", [P, NH])
        sel3 = sb("sel3", [3 * NH, NH * NS], BF16)
        coef = sb("coef", [P, NH * NS])
        a_ch = sb("a_ch", [P, G])
        band = sb("band", [P, 60])
        ident = sb("ident", [P, P])
        causal = sb("causal", [P, L])
        one = sb("one", [P, 1])
        a_exp = sb("a_exp", [P, NS])
        ln_stats = sb("ln_stats", [P, TT, 6])
        ln_mv = sb("ln_mv", [P, TT, 2])
        ln_rstd = sb("ln_rstd", [P, TT])
        xnT = sb("xnT", [P, T])
        x1 = xnT[:, :].rearrange("p (i d) -> p i d", d=DM)
        x4 = sb("x4", [P, TB])
        xt = sb("xt", [P, 2, DM])
        raw = sb("raw", [P, NQ, GC, L])
        x4b = sb("x4b", [3 * NH, TB], BF16)
        rt = sb("rt", [P, TB])
        rt_hi = sb("rt_hi", [P, TB], BF16)
        rt_mid = sb("rt_mid", [P, TB], BF16)
        rt_lo = sb("rt_lo", [P, TB], BF16)
        rt3 = sb("rt3", [3 * NH, NQ, TB], BF16)
        pd = sb("pd", [P, GC, L + 1])
        pi = sb("pi", [P, GC, L + 1])
        bt = sb("bt", [P, GC, L + 1])
        alpha = sb("alpha", [P, GC, L])
        rec_t = sb("rec_t", [P, 2, 2, HG])
        Z = sb("Z", [P, 2, GC, L + 1])
        S = sb("S", [P, 2, GC, L + 1])
        E = sb("E", [P, 2, GC, L])
        C = sb("C", [P, 2, GC, L])
        psi_end = sb("psi_end", [P, 2, 2, G, CH])
        VR = sb("VR", [P, 2, TB + KC - 1])
        V = sb("V", [P, 2, TB])
        GS = sb("GS", [P, 2, TB])
        YG = sb("YG", [P, 2, TB])
        carry = sb("carry", [P, 2, G, DH])
        st_t = sb("st_t", [P, 2, G, DH])
        st_z = sb("st_z", [P, 2, G, DH])
        st_s = sb("st_s", [P, 2, G, DH])
        vb = sb("vb", [P, 2, 2, G, 4 * DH])
        VT = YG[:, :, :].rearrange("p a (c l) -> p a c l", l=L)
        raw_flat = raw[:, :].rearrange("p q a l -> p q (a l)")
        kraw = [raw_flat[:, 0, 1024 * gh:1024 * gh + 512].rearrange("p (a m) -> p a m", m=4 * DH) for gh in range(2)]
        kin = raw_flat[:, 2, 0:1024].rearrange("p (c k g d) -> p c k g d", c=CH, k=2, g=G)
        hist = raw_flat[:, 3, 0:1024].rearrange("p (c k g d) -> p c k g d", c=CH, k=2, g=G)
        st = [carry] + [hist[:, c] for c in range(1, CH)] + [carry]
        GM = raw[:, 0]
        ub = raw[:, 1]
        ET = raw[:, 2:4]
        sq = C[:, 0].rearrange("p a b -> p (a b)").rearrange("p (k c) -> p k c", k=2)
        xT4 = raw[:, 0].rearrange("p a b -> p (a b)")
        xres = raw[:, 2].rearrange("p a b -> p (a b)")
        xsplit = [raw[:, 1].rearrange("p a b -> p (a b)").bitcast(BF16)[:, T * k:T * k + T] for k in range(2)]
        xsplit.append(raw[:, 3].rearrange("p a b -> p (a b)").bitcast(BF16)[:, 0:T])
        xin = E[:, 0].rearrange("p a b -> p (a b)").rearrange("p (i d) -> p i d", d=DM)
        par = C[:, :].rearrange("p a b c -> p (a b c)")[:, 0:TT * 4 * NH].rearrange("p (i k h) -> p i k h", k=4, h=NH)
        tmpf = C[:, :].rearrange("p a b c -> p (a b c)")[:, 2048:4096].rearrange("p (k i h) -> p k i h", k=4, h=NH)
        wv = w_bc[:, :, :].rearrange("p a b -> p (a b)")
        w1 = wv[:, 0:FF]
        w2 = wv[:, FF:2 * FF].rearrange("p (b o) -> p b o", b=4)
        b2b = wv[:, 1024:1152]
        b1 = wv[:, 1152:1156]
        scale = wv[:, 1156:1157]
        lt = wv[:, 1280:1280 + 16 * DM]
        hT = wv[:, 4096:4096 + 2 * 4 * FT].rearrange("p (k b t) -> p k b t", k=2, b=4)
        xn2 = E[:, 0].rearrange("p a b -> p (a b)").rearrange("p (i d) -> p i d", d=DM)
        xn2T = E[:, 1].rearrange("p a b -> p (a b)")
        yout = C[:, 0].rearrange("p a b -> p (a b)").rearrange("p (i d) -> p i d", d=DM)

        ps = ctx.enter_context(nc.psum_tensor("ps", [P, 8, 512], F32))
        psf = ps[:, :, :].rearrange("p b c -> p (b c)")

        def slot(gh):
            return psf[:, 1024 * gh:1024 * gh + 1024]

        def slot3(gh):
            return slot(gh).rearrange("p (a l) -> p a l", l=L)

        w_loaded = sem("w_loaded")
        x_loaded = sem("x_loaded")
        xt_loaded = sem("xt_loaded")
        zeroed = sem("zeroed")
        pro = sem("pro")
        pro_act = sem("pro_act")
        pro_pe = sem("pro_pe")
        x4_stored = sem("x4_stored")
        x4_ready = sem("x4_ready")
        coef_mm = sem("coef_mm")
        d_out = sem("d_out")
        pd_ready = sem("pd_ready")
        ln_ready = sem("ln_ready")
        pi_ready = sem("pi_ready")
        newton = sem("newton")
        coef_used = sem("coef_used")
        rec_m = sem("rec_m")
        rec_a = sem("rec_a")
        val_mm = sem("val_mm")
        vr_ready = sem("vr_ready")
        gate_ready = sem("gate_ready")
        conv_step = sem("conv_step")
        tail_ready = sem("tail_ready")
        v_ready = sem("v_ready")
        vt_ready = sem("vt_ready")
        w_mm = sem("w_mm")
        sq_ready = sem("sq_ready")
        raw_ready = sem("raw_ready")
        nrm_mm = sem("nrm_mm")
        root = sem("root")
        rt_step = sem("rt_step")
        rt3_ready = sem("rt3_ready")
        r_mm = sem("r_mm")
        normed = sem("normed")
        ec = sem("ec")
        ec_pool = sem("ec_pool")
        et_ready = sem("et_ready")
        psi_ready = sem("psi_ready")
        ub_zero = sem("ub_zero")
        ub_ready = sem("ub_ready")
        begun = sem("begun")
        clearing = sem("clearing")
        g_mm = sem("g_mm")
        gm_ready = sem("gm_ready")
        k_mm = sem("k_mm")
        kraw_ready = sem("kraw_ready")
        kin_ready = sem("kin_ready")
        st_step = sem("st_step")
        st_ready = sem("st_ready")
        vb_ready = sem("vb_ready")
        y_mm = sem("y_mm")
        yg_step = sem("yg_step")
        out_mm = sem("out_mm")
        x1_ready = sem("x1_ready")
        ffn_w = sem("ffn_w")
        lt_moved = sem("lt_moved")
        fv = sem("fv")
        fa = sem("fa")
        fp = sem("fp")
        h_mm = sem("h_mm")
        h_ready = sem("h_ready")
        o_mm = sem("o_mm")
        o_step = sem("o_step")
        stored = sem("stored")

        REC = 2 * 2 * L
        EC = 22
        RT = 7
        PRO_XN = 2 * TT + 2 + 1
        PRO_EXP = 2 * TT + 2 + TT + 3
        PRO_PAR = PRO_EXP + 21
        PRO_SPLIT = PRO_PAR + 4
        PRO_ACT = 1 + 4 + 3 + 4
        FV_XN = 4 + TT
        block = ctx.enter_context(nc.Block())
        loads = [(w_in, a["w_in"]), (coef, a["sel"]), (a_ch, a["A_ch"]), (band, a["band"]), (ident, a["ident"]),
                 (causal, a["causal"]), (conv_w, a["conv_w"]), (conv_b, a["conv_b"]), (skip, a["skip"]),
                 (w_out, a["w_out"])]
        NLOAD = len(loads) + 7

        @block.sync
        def _(sp):
            sp.dma_start(xin, a["x"].rearrange("(i p) d -> p i d", p=P)).then_inc(x_loaded, 16)
            for dst, src in loads:
                full = dst[:, :] if len(dst.shape) == 2 else dst[:, :, :]
                sp.dma_start(full, src).then_inc(w_loaded, 16)
            sp.dma_start(dt_bias[:, :], a["dt_bias"].partition_broadcast(P)).then_inc(w_loaded, 16)
            for r in range(0, P, NH):
                sp.dma_start(a_exp[r:r + 32, :], a["A_log"]).then_inc(w_loaded, 16)
            for half in range(2):
                sp.dma_start(w_bc[:, half, :], a["w_bc"][half]).then_inc(w_loaded, 16)
            xtiles = a["x"].rearrange("(b i p) d -> b p i d", i=2, p=P)

            x4_dram = a["x4"]
            sp.wait_ge(pro_act, PRO_ACT)
            sp.dma_start(x4_dram, xT4).then_inc(x4_stored, 16)
            sp.wait_ge(x4_stored, 16)
            x4_blocks = x4_dram.rearrange("p (b t) -> b p t", t=TB)

            for k in range(3):
                if k == 0:
                    sp.wait_ge(pro, PRO_SPLIT)
                sp.dma_start(a["x4b"][NH * k:NH * k + NH, :], xsplit[k][0:NH, :]).then_inc(x4_stored, 16)
            sp.wait_ge(x4_stored, 64)
            x4b_blocks = a["x4b"].rearrange("p (b t) -> b p t", t=TB)

            def block_rows(b):
                sp.dma_start(x4[:, :], x4_blocks[b]).then_inc(x4_ready, 16)
                sp.dma_start(x4b[:, :], x4b_blocks[b]).then_inc(x4_ready, 16)
                sp.wait_ge(x_loaded, 16)
                sp.wait_ge(x1_ready, b + 1)
                sp.dma_start(xt[:, :, :], xtiles[b]).then_inc(xt_loaded, 16)

            def scale_rows(b):
                for k, part in enumerate((rt_hi, rt_mid, rt_lo)):
                    sp.wait_ge(rt_step, RT * b + (4, 6, 7)[k])
                    for q in range(NQ):
                        sp.dma_start(rt3[NH * k:NH * k + NH, q, :],
                                     part[NH * q:NH * q + NH, :]).then_inc(rt3_ready, 16)

            block_rows(0)
            scale_rows(0)
            with sp.Fori(1, NB) as b:
                sp.wait_ge(x4_stored, 64)
                sp.wait_ge(coef_used, 10 * b)
                block_rows(b)
                scale_rows(b)
            sp.wait_ge(w_mm, 8 * NB)
            sp.dma_start(w1, a["w1"]).then_inc(ffn_w, 16)
            sp.dma_start(w2, a["w2"]).then_inc(ffn_w, 16)
            sp.dma_start(b2b, a["b2"].partition_broadcast(P)).then_inc(ffn_w, 16)
            sp.dma_start(b1, a["b1"]).then_inc(ffn_w, 16)
            sp.dma_start(scale, a["scale"].partition_broadcast(P)).then_inc(ffn_w, 16)
            sp.wait_ge(fv, FV_XN)
            sp.dma_start(lt[0:1, :].rearrange("o (t d) -> o t d", d=DM), xn2[1:17, 0, :]).then_inc(lt_moved, 16)
            yd = a["y"].rearrange("(i p) d -> p i d", p=P)
            for f in range(FG):
                sp.wait_ge(o_step, 2 * (f + 1))
                sp.dma_start(yd[:, 4 * f:4 * f + 4, :], yout[:, 4 * f:4 * f + 4, :]).then_inc(stored, 16)
            sp.wait_ge(stored, 16 * FG)

        @block.tensor
        def _(pe):
            def d_rows(b):
                pe.wait_ge(x4_ready, 32 * b + 32)
                pe.wait_ge(normed, 8 * b)
                for gh in range(2):
                    for g4 in range(4):
                        g = 4 * gh + g4
                        mm = pe.matmul(slot(gh)[:, TB * g4:TB * g4 + TB], coef[:, P * g:P * g + P], x4[:, :],
                                       start=True, stop=True)
                    mm.then_inc(coef_mm, 1)

            def dt_rows(b):
                for gh in range(2):
                    pe.wait_ge(d_out, 2 * b + gh + 1)
                    for g4 in range(4):
                        g = 4 * gh + g4
                        mm = pe.matmul(slot(gh)[:, TB * g4:TB * g4 + TB], sel3[:, P * g:P * g + P], x4b[:, :],
                                       start=True, stop=True)
                    mm.then_inc(coef_mm, 1)

            def value_gate(b):
                pe.wait_ge(gm_ready, 8 * b)
                for k in range(2):
                    for half in range(2):
                        col = DI * k + P * half
                        mm = pe.matmul(ps[:, 6 + k, TB * half:TB * half + TB], w_in[:, col:col + P],
                                       xnT[:, bass.ts(b, TB)], start=True, stop=True)
                    mm.then_inc(val_mm, 1)

            def bc_products(b):
                def sums(k):
                    q, gh = k // 2, k % 2
                    pe.wait_ge(sq_ready, 8 * b + k + 1)
                    for g4 in range(4):
                        g = 4 * gh + g4
                        mm = pe.matmul(ps[32 * q:32 * q + 32, 4, 0:TB], band[:, 28 - 4 * g:60 - 4 * g],
                                       sq[:, k % 2, TB * g4:TB * g4 + TB], start=(g == 0), stop=(g == G - 1))
                    mm.then_inc(nrm_mm, 1)

                pe.wait_ge(v_ready, 2 * b + 2)
                pe.wait_ge(coef_used, 10 * b + 10)
                pe.wait_ge(yg_step, 3 * b)
                for k in range(8):
                    q, gh = k // 2, k % 2
                    if k >= 2:
                        pe.wait_ge(raw_ready, 8 * b + k - 1)
                    for g4 in range(4):
                        col = (q * G + 4 * gh + g4) * P
                        for half in range(2):
                            mm = pe.matmul(slot(gh)[:, TB * g4:TB * g4 + TB], w_bc[:, half, col:col + P],
                                           V[:, half, :], start=(half == 0), stop=(half == 1))
                    mm.then_inc(w_mm, 1)
                    if k >= 1:
                        sums(k - 1)
                sums(7)

            def scales(b):
                pe.wait_ge(raw_ready, 8 * b + 8)
                pe.wait_ge(rt3_ready, 192 * (b + 1))
                for k in range(8):
                    gh, q = k // 4, k % 4
                    if k >= 2:
                        pe.wait_ge(normed, 8 * b + k - 1)
                    for g4 in range(4):
                        g = 4 * gh + g4
                        mm = pe.matmul(slot(k % 2)[:, TB * g4:TB * g4 + TB], sel3[:, P * g:P * g + P], rt3[:, q, :],
                                       start=True, stop=True)
                    mm.then_inc(r_mm, 1)

            def scores(b, gh):
                pe.wait_ge(ec, EC * b + 11 * gh + 11)
                pe.wait_ge(ec_pool, 6 * b + 3 * gh + 3)
                pe.wait_ge(kraw_ready, 2 * b + gh + 1)
                if gh == 0:
                    pe.wait_ge(x1_ready, b + 1)
                    pe.wait_ge(vr_ready, b + 1)
                    pe.wait_ge(gate_ready, b + 1)
                else:
                    pe.wait_ge(gm_ready, 8 * b + 4)
                pe.sem_inc(begun, 1)
                for m in range(HG // 4):
                    for r in range(4):
                        for comp in range(2):
                            for j in range(4):
                                bank = (j + r) % 4
                                gc = HG * gh + (HG // 4) * bank + m
                                rows = slice(32 * j, 32 * j + 32)
                                mm = pe.matmul(ps[rows, 4 + bank, L * m:L * m + L], E[rows, comp, gc, :],
                                               C[rows, comp, gc, :], start=(comp == 0), stop=(comp == 1))
                mm.then_inc(g_mm, 1)

            def chunk_inputs(b, gh):
                pe.wait_ge(et_ready, 4 * b + 2 * gh + 2)
                pe.wait_ge(ub_ready, 32 * b + 16 * gh + 16)
                if gh == 0:
                    pe.wait_ge(root, b + 1)
                else:
                    pe.wait_ge(gm_ready, 8 * b + 4)
                pe.sem_inc(begun, 1)
                for c in range(CH):
                    for comp in range(2):
                        for g4 in range(4):
                            gc = (4 * gh + g4) * CH + c
                            col = 4 * DH * (2 * c + comp)
                            mm = pe.matmul(ps[32 * g4:32 * g4 + 32, 4, col:col + 4 * DH], ET[:, comp, gc, :],
                                           ub[:, gc, :], start=True, stop=True)
                mm.then_inc(k_mm, 1)

            def outputs(b):
                pe.wait_ge(gm_ready, 8 * b + 8)
                for c in range(CH):
                    pe.wait_ge(vb_ready, 32 * b + 4 * c + 5)
                    for g in range(G):
                        gc = g * CH + c
                        out = ps[32 * (g % 4):32 * (g % 4) + 32, 4, (g // 4) * TB + c * L:(g // 4) * TB + c * L + L]
                        pe.matmul(out, ub[:, gc, :], GM[:, gc, :], start=True, stop=False)
                        pe.matmul(out, vb[:, c % 2, 0, g, :], C[:, 0, gc, :], start=False, stop=False)
                        mm = pe.matmul(out, vb[:, c % 2, 1, g, :], C[:, 1, gc, :], start=False, stop=True)
                    mm.then_inc(y_mm, 1)
                pe.wait_ge(yg_step, 3 * b + 3)
                for i in range(2):
                    for half in range(2):
                        mm = pe.matmul(ps[:, 5, DM * i:DM * i + DM], YG[:, half, P * i:P * i + P], w_out[:, half, :],
                                       start=(half == 0), stop=(half == 1))
                mm.then_inc(out_mm, 1)

            pe.wait_ge(w_loaded, 16 * NLOAD)
            for i in range(TT):
                pe.wait_ge(pro, PRO_XN + i)
                pe.transpose(psf[:, DM * i:DM * i + DM], xin[:, i, :], ident[:, :]).then_inc(pro_pe, 1)
            for i in range(TT):
                pe.wait_ge(pro_act, 1 + i // 4 + 1)
                mm = pe.matmul(psf[:, 2048 + 64 * i:2048 + 64 * i + 64], xnT[:, P * i:P * i + P],
                               w_in[:, 2 * DI:], start=True, stop=True)
            mm.then_inc(pro_pe, 1)
            pe.wait_ge(pro, PRO_PAR)
            for i in range(TT):
                mm = pe.transpose(psf[:, P * i:P * i + P], par[:, i].rearrange("p k h -> p (k h)"), ident[:, :])
            mm.then_inc(pro_pe, 1)
            pe.wait_ge(pro_act, PRO_ACT)

            d_rows(0)
            dt_rows(0)
            value_gate(0)
            bc_products(0)
            scales(0)
            with pe.Fori(1, NB) as b:
                d_rows(b)
                chunk_inputs(b - 1, 0)
                scores(b - 1, 0)
                dt_rows(b)
                chunk_inputs(b - 1, 1)
                scores(b - 1, 1)
                outputs(b - 1)
                value_gate(b)
                bc_products(b)
                scales(b)
            for gh in range(2):
                chunk_inputs(NB - 1, gh)
                scores(NB - 1, gh)
            outputs(NB - 1)

            for i in range(TT):
                pe.wait_ge(fv, 4 + i + 1)
                pe.transpose(psf[:, DM * i:DM * i + DM], xn2[:, i, :], ident[:, :]).then_inc(fp, 1)
            pe.wait_ge(lt_moved, 16)
            pe.wait_ge(x1_ready, NB + 1)

            def token(t, lo=0, n=DM, step=1):
                return lt[0:1, (t - 1) * DM + lo:(t - 1) * DM + lo + (n - 1) * step + 1:step]
            for r in range(4):
                pe.matmul(ps[:, 4, DM * r:DM * r + DM], token(2 + 2 * r), token(1 + 2 * r), start=True, stop=True)
            for q in range(4):
                for r in range(4):
                    mm = pe.matmul(ps[:, 5, DM * q + 32 * r:DM * q + 32 * r + 32], token(10 + 2 * r),
                                   token(9 + 2 * r, q, 32, 4), start=True, stop=True)
            mm.then_inc(fp, 1)

            def hidden(f):
                for hb in range(4):
                    pe.wait_ge(fa, f + 2)
                    pe.wait_ge(fv, FV_XN + 3)
                    k = 4 * f + hb
                    if k >= 2:
                        pe.wait_ge(h_ready, k - 1)
                    pe.matmul(ps[:, 6 + k % 2, :], w1[:, P * hb:P * hb + P], xn2T[:, FT * f:FT * f + FT],
                              start=True, stop=True).then_inc(h_mm, 1)

            def back(f):
                pe.wait_ge(h_ready, 4 * f + 4)
                if f >= 2:
                    pe.wait_ge(o_step, 2 * f - 3)
                for i in range(4):
                    for hb in range(4):
                        mm = pe.matmul(ps[:, 4 + f % 2, DM * i:DM * i + DM], hT[:, f % 2, hb, P * i:P * i + P],
                                       w2[:, hb, :], start=(hb == 0), stop=(hb == 3))
                mm.then_inc(o_mm, 1)

            hidden(0)
            for f in range(FG):
                if f + 1 < FG:
                    hidden(f + 1)
                back(f)

        @block.scalar
        def _(act):
            def d_copies(b):
                for gh in range(2):
                    act.wait_ge(coef_mm, 4 * b + gh + 1)
                    if gh == 0:
                        act.wait_ge(rec_a, REC * b)
                    act.activation(bt[:, HG * gh:HG * gh + HG, 1:], slot3(gh), ACT.Copy).then_inc(d_out, 1)

            def inverse_products(b):
                act.wait_ge(pd_ready, b + 1)
                act.activation(bt[:, :, 1:], pd[:, :, 1:], ACT.Ln).then_inc(ln_ready, 1)
                act.wait_ge(ln_ready, b + 1)
                act.activation(pi[:, :, 1:], bt[:, :, 1:], ACT.Exp, scale=-1.0).then_inc(pi_ready, 1)

            def front(b):
                act.wait_ge(val_mm, 2 * b + 1)
                act.wait_ge(tail_ready, b + 1)
                act.activation(VR[:, :, KC - 1:], ps[:, 6, :].rearrange("p (h t) -> p h t", h=2),
                               ACT.Copy).then_inc(vr_ready, 1)
                act.wait_ge(val_mm, 2 * b + 2)
                act.wait_ge(yg_step, 3 * b)
                act.activation(GS[:, :, :], ps[:, 7, :].rearrange("p (h t) -> p h t", h=2),
                               ACT.Silu).then_inc(gate_ready, 1)
                act.wait_ge(conv_step, 8 * b + 8)
                for half in range(2):
                    act.activation(V[:, half, :], YG[:, half, :], ACT.Silu,
                                   bias=conv_b[:, half:half + 1]).then_inc(v_ready, 1)
                for k in range(8):
                    q, gh = k // 2, k % 2
                    act.wait_ge(w_mm, 8 * b + k + 1)
                    if k >= 2:
                        act.wait_ge(nrm_mm, 8 * b + k - 1)
                    if k == 4:
                        act.wait_ge(st_ready, 16 * b + 1)
                    act.activation(sq[:, k % 2, :], slot(gh), ACT.Square).then_inc(sq_ready, 1)
                    act.activation(raw[:, q, HG * gh:HG * gh + HG, :], slot3(gh), ACT.Copy).then_inc(raw_ready, 1)
                act.wait_ge(nrm_mm, 8 * b + 8)
                act.activation(rt[:, :], ps[:, 4, 0:TB], ACT.Sqrt).then_inc(root, 1)

            def values(b, gh):
                act.wait_ge(ub_zero, 2 * b + gh + 1)
                act.wait_ge(vt_ready, b + 1)
                for j in range(4):
                    for g4 in range(4):
                        gc = (4 * gh + g4) * CH
                        act.activation(ub[32 * j:32 * j + 32, gc:gc + CH, DH * j:DH * j + DH],
                                       VT[32 * g4:32 * g4 + 32, gh, :, DH * j:DH * j + DH],
                                       ACT.Copy).then_inc(ub_ready, 1)

            def input_copy(b, gh):
                act.wait_ge(k_mm, 2 * b + gh + 1)
                act.activation(kraw[gh], ps[:, 4, :].rearrange("p (a m) -> p a m", m=4 * DH),
                               ACT.Copy).then_inc(kraw_ready, 1)

            def input_moves(b, gh):
                act.wait_ge(kraw_ready, 2 * b + gh + 1)
                for j in range(4):
                    for g4 in range(4):
                        act.activation(kin[32 * j:32 * j + 32, :, :, 4 * gh + g4, :].rearrange("p c k d -> p (c k) d"),
                                       kraw[gh][32 * g4:32 * g4 + 32, :, DH * j:DH * j + DH],
                                       ACT.Copy).then_inc(kin_ready, 1)

            def spread_states(b):
                for c in range(CH):
                    act.wait_ge(st_ready, 16 * b + 2 * c + 1)
                    if c >= 2:
                        act.wait_ge(y_mm, 8 * b + c - 1)
                    for j in range(4):
                        rows = slice(32 * j, 32 * j + 32)
                        act.activation(vb[rows, c % 2, :, :, DH * j:DH * j + DH], st[c][rows],
                                       ACT.Copy).then_inc(vb_ready, 1)

            act.wait_ge(pro, 2 * TT + 1)
            act.activation(ln_rstd[:, :], ln_mv[:, :, 1], ACT.Sqrt).then_inc(pro_act, 1)
            for k in range(4):
                act.wait_ge(pro_pe, 4 * k + 4)
                act.activation(xnT[:, 512 * k:512 * k + 512], ps[:, k, :], ACT.Copy).then_inc(pro_act, 1)
            act.wait_ge(w_loaded, 16 * NLOAD)
            act.wait_ge(pro, PRO_EXP)
            act.activation(tmpf[:, 0:2], tmpf[:, 2:4], ACT.Exp).then_inc(pro_act, 1)
            act.activation(a_exp[:, :], a_exp[:, :], ACT.Exp).then_inc(pro_act, 1)
            act.activation(a_ch[:, :], a_ch[:, :], ACT.Exp).then_inc(pro_act, 1)
            act.wait_ge(pro_pe, TT + 2)
            for k in range(4):
                act.activation(xT4[:, 512 * k:512 * k + 512], ps[:, k, :], ACT.Copy).then_inc(pro_act, 1)
            d_copies(0)
            inverse_products(0)
            front(0)
            values(0, 0)
            with act.Fori(1, NB) as b:
                d_copies(b)
                input_copy(b - 1, 0)
                input_moves(b - 1, 0)
                values(b - 1, 1)
                inverse_products(b)
                input_copy(b - 1, 1)
                input_moves(b - 1, 1)
                spread_states(b - 1)
                front(b)
                values(b, 0)
            input_copy(NB - 1, 0)
            input_moves(NB - 1, 0)
            values(NB - 1, 1)
            input_copy(NB - 1, 1)
            input_moves(NB - 1, 1)
            spread_states(NB - 1)

            act.wait_ge(fv, 2)
            act.activation(ln_rstd[:, :], ln_mv[:, :, 1], ACT.Sqrt).then_inc(fa, 1)
            for k in range(FG):
                act.wait_ge(fp, 4 * k + 4)
                act.activation(xn2T[:, 512 * k:512 * k + 512], ps[:, k, :], ACT.Copy).then_inc(fa, 1)
            for k in range(4 * FG):
                f, hb = k // 4, k % 4
                act.wait_ge(h_mm, k + 1)
                if hb == 0 and f >= 2:
                    act.wait_ge(o_mm, f - 1)
                act.activation(hT[:, f % 2, hb, :], ps[:, 6 + k % 2, :], ACT.Gelu,
                               bias=b1[:, hb:hb + 1]).then_inc(h_ready, 1)

        @block.gpsimd
        def _(pool):
            def sums(b, gh):
                r = slice(HG * gh, HG * gh + HG)
                pool.wait_ge(ec, EC * b + 11 * gh + 4)
                pool.tensor_tensor(E[:, 1, r], C[:, 0, r], E[:, 1, r], ALU.subtract).then_inc(ec_pool, 1)
                pool.wait_ge(ec, EC * b + 11 * gh + 6)
                pool.tensor_tensor(E[:, 0, r], E[:, 0, r], C[:, 1, r], ALU.subtract).then_inc(ec_pool, 1)
                pool.wait_ge(ec, EC * b + 11 * gh + 9)
                pool.tensor_tensor(C[:, 0, r], C[:, 0, r], raw[:, 0, r], ALU.add).then_inc(ec_pool, 1)
                pool.wait_ge(ec, EC * b + 11 * gh + 11)
                pool.sem_inc(clearing, 1)
                pool.memset(ub[:, r], 0.0).then_inc(ub_zero, 1)

            def states(b):
                pool.wait_ge(kin_ready, 32 * b + 32)
                pool.wait_ge(psi_ready, 2 * b + 2)
                for c in range(CH):
                    pool.wait_ge(st_ready, 16 * b + 2 * c + 1)
                    pool.tensor_tensor(st_t[:, :], st[c][:, :], kin[:, c], ALU.add).then_inc(st_step, 1)
                    pool.wait_ge(st_step, 24 * b + 3 * c + 1)
                    for i, dst in enumerate((st_z, st_s)):
                        m = psi_end[:, i, :, :, c].unsqueeze(3).broadcast_to([P, 2, G, DH])
                        pool.tensor_tensor(dst[:, :], st_t[:, :], m, ALU.mult).then_inc(st_step, 1)
                    if c == CH - 1:
                        pool.wait_ge(vb_ready, 32 * b + 5)
                    for i, src in enumerate((st_z, st_s)):
                        pool.wait_ge(st_step, 24 * b + 3 * c + 2 + i)
                        pool.tensor_tensor(st[c + 1][:, i], src[:, 0], src[:, 1], ALU.add).then_inc(st_ready, 1)

            pool.memset(bt[:, :, 0:1], 0.0).then_inc(zeroed, 1)
            pool.memset(VR[:, :, 0:KC - 1], 0.0).then_inc(zeroed, 1)
            pool.memset(carry[:, :], 0.0).then_inc(st_ready, 1)
            pool.memset(vb[:, :], 0.0).then_inc(vb_ready, 1)
            pool.memset(Z[:, 0, :, 0:1], 1.0).then_inc(zeroed, 1)
            pool.memset(Z[:, 1, :, 0:1], 0.0).then_inc(zeroed, 1)
            pool.memset(S[:, 0, :, 0:1], 0.0).then_inc(zeroed, 1)
            pool.memset(S[:, 1, :, 0:1], 1.0).then_inc(zeroed, 1)
            pool.memset(one[:, :], 1.0).then_inc(zeroed, 1)
            pool.wait_ge(zeroed, 7)
            pool.wait_ge(pro_act, PRO_ACT)
            for gh in range(2):
                sums(0, gh)
            with pool.Fori(1, NB) as b:
                states(b - 1)
                for gh in range(2):
                    sums(b, gh)
            states(NB - 1)

        @block.vector
        def _(dve):
            def coefficients(b, between):
                dve.wait_ge(d_out, 2 * b + 2)
                dve.tensor_tensor_scan(pd[:, :, :].rearrange("p a l -> p (a l)"), bt[:, :, :].rearrange("p a l -> p (a l)"),
                                       one[:, 0:1].broadcast_to([P, GC * (L + 1)]), 1.0, ALU.mult, ALU.max
                                       ).then_inc(pd_ready, 1)
                between()
                dve.wait_ge(pi_ready, b + 1)
                dve.tensor_tensor(bt[:, :, 1:], pd[:, :, 1:], pi[:, :, 1:], ALU.mult).then_inc(newton, 1)
                for g in range(G):
                    r = slice(CH * g, CH * g + CH)
                    if g % 4 == 0:
                        dve.wait_ge(coef_mm, 4 * b + 3 + g // 4)
                    dve.scalar_tensor_tensor(out=alpha[:, r], in0=slot3(g // 4)[:, CH * (g % 4):CH * (g % 4) + CH],
                                             scalar=a_ch[:, g:g + 1], in1=pd[:, r, 0:L], op0=ALU.mult,
                                             op1=ALU.mult).then_inc(coef_used, 1)
                dve.wait_ge(newton, 2 * b + 1)
                dve.scalar_tensor_tensor(out=pi[:, :, 1:], in0=bt[:, :, 1:], scalar=2.0, in1=pi[:, :, 1:],
                                         op0=ALU.subtract, op1=ALU.mult, reverse0=True).then_inc(newton, 1)
                dve.wait_ge(newton, 2 * b + 2)
                for gh in range(2):
                    r = slice(HG * gh, HG * gh + HG)
                    dve.tensor_tensor(bt[:, r, 1:], slot3(gh), pi[:, r, 1:], ALU.mult).then_inc(coef_used, 1)

            def recursion(b, between):
                dve.wait_ge(coef_used, 10 * b + 10)
                for k in range(L):
                    if k == 8:
                        between()
                    for i, (coefs, src, dst) in enumerate(((alpha[:, :, k], S[:, :, :, k], Z),
                                                           (bt[:, :, k + 1], Z[:, :, :, k + 1], S))):
                        n = 4 * k + 2 * i
                        for gh in range(2):
                            r = slice(HG * gh, HG * gh + HG)
                            if n:
                                dve.wait_ge(rec_a, REC * b + n - 2 + gh + 1)
                            m = coefs[:, r].unsqueeze(1).broadcast_to([P, 2, HG])
                            dve.tensor_tensor(rec_t[:, gh], m, src[:, :, r], ALU.mult).then_inc(rec_m, 1)
                        for gh in range(2):
                            r = slice(HG * gh, HG * gh + HG)
                            dve.wait_ge(rec_m, REC * b + n + gh + 1)
                            dve.tensor_tensor(dst[:, :, r, k + 1], dst[:, :, r, k], rec_t[:, gh],
                                              ALU.add if i else ALU.subtract).then_inc(rec_a, 1)

            def convolution(b):
                dve.wait_ge(vr_ready, b + 1)
                for half in range(2):
                    dve.tensor_scalar(YG[:, half, :], VR[:, half, 0:TB], conv_w[:, half, 0:1], None,
                                      ALU.mult).then_inc(conv_step, 1)
                for k in range(1, KC):
                    for half in range(2):
                        dve.wait_ge(conv_step, 8 * b + 2 * (k - 1) + half + 1)
                        dve.scalar_tensor_tensor(out=YG[:, half, :], in0=VR[:, half, k:k + TB],
                                                 scalar=conv_w[:, half, k:k + 1], in1=YG[:, half, :],
                                                 op0=ALU.mult, op1=ALU.add).then_inc(conv_step, 1)
                dve.wait_ge(conv_step, 8 * b + 8)
                dve.tensor_copy(VR[:, :, 0:KC - 1], VR[:, :, TB:]).then_inc(tail_ready, 1)
                dve.wait_ge(v_ready, 2 * b + 2)
                dve.transpose(VT[:, :].rearrange("p a b c -> p (a b c)"),
                              V[:, :, :].rearrange("p a b -> p (a b)")).then_inc(vt_ready, 1)

            def row_scales(b):
                dve.wait_ge(root, b + 1)
                dve.wait_ge(x4_ready, 32 * b + 32)
                n = RT * b
                dve.tensor_scalar(rt[:, :], rt[:, :], NORM_EPS, None, ALU.add).then_inc(rt_step, 1)
                dve.wait_ge(rt_step, n + 1)
                dve.reciprocal(rt[:, :], rt[:, :]).then_inc(rt_step, 1)
                dve.wait_ge(rt_step, n + 2)
                dve.tensor_tensor(rt[0:64, :], rt[0:64, :], x4[0:64, :], ALU.mult).then_inc(rt_step, 1)
                dve.wait_ge(rt_step, n + 3)
                dve.wait_ge(r_mm, 8 * b)
                dve.tensor_copy(rt_hi[:, :], rt[:, :]).then_inc(rt_step, 1)
                dve.wait_ge(rt_step, n + 4)
                dve.tensor_tensor(rt[:, :], rt[:, :], rt_hi[:, :], ALU.subtract).then_inc(rt_step, 1)
                dve.wait_ge(rt_step, n + 5)
                dve.tensor_copy(rt_mid[:, :], rt[:, :]).then_inc(rt_step, 1)
                dve.wait_ge(rt_step, n + 6)
                dve.tensor_tensor(rt_lo[:, :], rt[:, :], rt_mid[:, :], ALU.subtract).then_inc(rt_step, 1)

            def chunk_operands(b, gh):
                r = slice(HG * gh, HG * gh + HG)
                for q in range(4):
                    dve.wait_ge(r_mm, 8 * b + 4 * gh + q + 1)
                    dve.tensor_tensor(raw[:, q, r], raw[:, q, r], slot3(q % 2), ALU.mult).then_inc(normed, 1)
                n, m = EC * b + 11 * gh, 6 * b + 3 * gh

                def step(out, x, y, op=ALU.mult, after=0):
                    if after:
                        dve.wait_ge(ec, n + after)
                    dve.tensor_tensor(out, x, y, op).then_inc(ec, 1)
                bz, bx, cz, cx = (raw[:, q, r] for q in range(4))
                p, q_, s_r, s_w = Z[:, 0, r, 1:], Z[:, 1, r, 1:], S[:, 0, r], S[:, 1, r]
                if gh == 0:
                    dve.wait_ge(rec_a, REC * b + REC)
                dve.wait_ge(normed, 8 * b + 4 * gh + 4)
                step(bz, bz, pd[:, r, 0:L])
                step(cz, cz, pi[:, r, 1:])
                step(C[:, 0, r], bx, p)
                step(E[:, 1, r], bz, s_r[:, :, 0:L], after=1)
                step(C[:, 1, r], bx, q_)
                step(E[:, 0, r], bz, s_w[:, :, 0:L])
                step(raw[:, 0, r], cx, s_r[:, :, 1:], after=6)
                step(raw[:, 1, r], cx, s_w[:, :, 1:])
                dve.wait_ge(ec_pool, m + 1)
                step(C[:, 0, r], cz, p, after=2)
                dve.wait_ge(ec_pool, m + 2)
                step(C[:, 1, r], cz, q_)
                for comp in (1, 0):
                    dve.wait_ge(ec, n + 10)
                    dve.transpose(ET[:, comp, r].rearrange("p a l -> p (a l)"),
                                  E[:, comp, r].rearrange("p a l -> p (a l)")).then_inc(et_ready, 1)
                step(C[:, 1, r], C[:, 1, r], raw[:, 1, r], ALU.add, after=10)
                if gh == 1:
                    dve.wait_ge(st_ready, 16 * b + 1)
                    pe2 = psi_end[:, :].rearrange("p i k g c -> p i k (g c)")
                    dve.tensor_tensor(pe2[:, 0], Z[:, :, :, L], pi[:, :, L].unsqueeze(1).broadcast_to([P, 2, GC]),
                                      ALU.mult).then_inc(psi_ready, 1)
                    dve.tensor_copy(pe2[:, 1], S[:, :, :, L]).then_inc(psi_ready, 1)

            def mask_scores(b, gh):
                dve.wait_ge(g_mm, 2 * b + gh + 1)
                dve.wait_ge(kin_ready, 32 * b + 16 * gh + 16)
                for i in range(4):
                    gc = HG * gh + 8 * i
                    dve.tensor_tensor(GM[:, gc:gc + 8, :], ps[:, 4 + i, 0:256].rearrange("p (a l) -> p a l", l=L),
                                      causal[:, :].unsqueeze(1).broadcast_to([P, 8, L]), ALU.mult).then_inc(gm_ready, 1)

            def gated(b):
                dve.wait_ge(y_mm, 8 * b + 8)
                for half in range(2):
                    dve.scalar_tensor_tensor(out=YG[:, half, :], in0=V[:, half, :], scalar=skip[:, half:half + 1],
                                             in1=ps[:, 4, TB * half:TB * half + TB], op0=ALU.mult,
                                             op1=ALU.add).then_inc(yg_step, 1)
                dve.wait_ge(yg_step, 3 * b + 2)
                dve.tensor_tensor(YG[:, :, :], YG[:, :, :], GS[:, :, :], ALU.mult).then_inc(yg_step, 1)
                dve.wait_ge(out_mm, b + 1)
                dve.wait_ge(xt_loaded, 16 * b + 16)
                dve.tensor_tensor(xnT[:, bass.ts(b, TB)], ps[:, 5, 0:TB], xt[:, :, :].rearrange("p i d -> p (i d)"),
                                  ALU.add).then_inc(x1_ready, 1)

            count = [0]

            def link(ins):
                count[0] += 1
                ins.then_inc(pro, 1)
                dve.wait_ge(pro, count[0])

            dve.wait_ge(x_loaded, 16)
            for i in range(TT):
                dve.bn_stats(ln_stats[:, i, :], xin[:, i, :]).then_inc(pro, 1)
            for i in range(TT):
                dve.wait_ge(pro, i + 1)
                dve.bn_aggr(ln_mv[:, i, :], ln_stats[:, i, :]).then_inc(pro, 1)
            count[0] = 2 * TT
            dve.wait_ge(pro, 2 * TT)
            link(dve.tensor_scalar(ln_mv[:, :, 1], ln_mv[:, :, 1], LN_EPS, None, ALU.add))
            dve.wait_ge(pro_act, 1)
            link(dve.reciprocal(ln_rstd[:, :], ln_rstd[:, :]))
            for i in range(TT):
                dve.tensor_scalar(xin[:, i, :], xin[:, i, :], ln_mv[:, i, 0:1], ln_rstd[:, i:i + 1],
                                  ALU.subtract, ALU.mult).then_inc(pro, 1)
            count[0] += TT
            dve.wait_ge(w_loaded, 16 * NLOAD)
            dve.wait_ge(pro, count[0])
            dve.wait_ge(pro_pe, TT + 1)
            pp = psf[:, 2048:3072].rearrange("p (i k h) -> p i k h", k=2, h=NH)
            dtb = dt_bias[:, :].unsqueeze(1).broadcast_to([P, TT, NH])
            link(dve.tensor_tensor(tmpf[:, 2], pp[:, :, 0], dtb, ALU.add))
            link(dve.tensor_scalar(tmpf[:, 2], tmpf[:, 2], 0.0, None, ALU.min))
            link(dve.tensor_scalar(tmpf[:, 3], pp[:, :, 1], -1.0, None, ALU.mult))
            assert count[0] == PRO_EXP
            dve.wait_ge(pro_act, 1 + 4 + 1)
            v, w, t2, t3 = (tmpf[:, k] for k in range(4))
            dt, dt_again, dt2, cc = (par[:, :, k] for k in range(4))
            link(dve.tensor_scalar(v, v, 0.11, None, ALU.min))
            link(dve.tensor_scalar(t2, v, 2.0, None, ALU.add))
            link(dve.reciprocal(t2, t2))
            link(dve.tensor_tensor(v, v, t2, ALU.mult))
            link(dve.tensor_tensor(t2, v, v, ALU.mult))
            link(dve.tensor_scalar(t3, t2, 2.0 / 7, 2.0 / 5, ALU.mult, ALU.add))
            link(dve.tensor_tensor(t3, t3, t2, ALU.mult))
            link(dve.tensor_scalar(t3, t3, 2.0 / 3, None, ALU.add))
            link(dve.tensor_tensor(t3, t3, t2, ALU.mult))
            link(dve.tensor_scalar(t3, t3, 2.0, None, ALU.add))
            link(dve.tensor_tensor(t3, t3, v, ALU.mult))
            link(dve.tensor_scalar(dt, t3, DT_MIN, DT_MAX, ALU.max, ALU.min))
            link(dve.tensor_copy(dt_again, dt))
            link(dve.tensor_tensor(dt2, dt, dt, ALU.mult))
            link(dve.tensor_scalar(w, w, 1.0, None, ALU.add))
            link(dve.reciprocal(w, w))
            link(dve.tensor_tensor(w, w, dt, ALU.mult))
            link(dve.tensor_scalar(cc, w, K_MAX, 1.0, ALU.mult, ALU.add))
            dve.wait_ge(pro_act, 1 + 4 + 3)
            link(dve.tensor_copy(sel3[:, :], coef[0:96, :]))
            link(dve.memset(coef[0:64, :], 0.0))
            rows = slice(64, 96)
            link(dve.tensor_tensor(coef[rows, :].rearrange("p (h n) -> p h n", n=NS),
                                   coef[rows, :].rearrange("p (h n) -> p h n", n=NS),
                                   a_exp[rows, :].unsqueeze(1).broadcast_to([32, NH, NS]), ALU.mult))
            assert count[0] == PRO_PAR, (count[0], PRO_PAR)
            dve.wait_ge(pro_act, PRO_ACT)
            link(dve.tensor_copy(xsplit[0][0:NH, :], xT4[0:NH, :]))
            link(dve.tensor_tensor(xres[0:NH, :], xT4[0:NH, :], xsplit[0][0:NH, :], ALU.subtract))
            link(dve.tensor_copy(xsplit[1][0:NH, :], xres[0:NH, :]))
            link(dve.tensor_tensor(xsplit[2][0:NH, :], xres[0:NH, :], xsplit[1][0:NH, :], ALU.subtract))
            dve.wait_ge(zeroed, 7)
            dve.tensor_copy(VR[:, :, 0:KC - 1], VR[:, :, 0:KC - 1]).then_inc(tail_ready, 1)
            dve.sem_inc(x1_ready, 1)

            coefficients(0, lambda: None)
            recursion(0, lambda: None)
            convolution(0)
            row_scales(0)
            for gh in range(2):
                chunk_operands(0, gh)
            with dve.Fori(1, NB) as b:
                coefficients(b, lambda: mask_scores(b - 1, 0))
                recursion(b, lambda: mask_scores(b - 1, 1))
                gated(b - 1)
                convolution(b)
                row_scales(b)
                for gh in range(2):
                    chunk_operands(b, gh)
            for gh in range(2):
                mask_scores(NB - 1, gh)
            gated(NB - 1)

            dve.wait_ge(x1_ready, NB + 1)
            for i in range(TT):
                ins = dve.bn_stats(ln_stats[:, i, :], x1[:, i, :])
                ins.then_inc(pro, 1)
            for i in range(TT):
                dve.wait_ge(pro, PRO_SPLIT + i + 1)
                dve.bn_aggr(ln_mv[:, i, :], ln_stats[:, i, :]).then_inc(pro, 1)
            dve.wait_ge(pro, PRO_SPLIT + 2 * TT)
            dve.tensor_scalar(ln_mv[:, :, 1], ln_mv[:, :, 1], LN_EPS, None, ALU.add).then_inc(fv, 2)
            dve.wait_ge(fa, 1)
            dve.reciprocal(ln_rstd[:, :], ln_rstd[:, :]).then_inc(fv, 2)
            dve.wait_ge(fv, 4)
            for i in range(TT):
                dve.tensor_scalar(xn2[:, i, :], x1[:, i, :], ln_mv[:, i, 0:1], ln_rstd[:, i:i + 1],
                                  ALU.subtract, ALU.mult).then_inc(fv, 1)
            dve.wait_ge(ffn_w, 16 * 5)
            dve.wait_ge(fp, TT + 1)
            dve.scalar_tensor_tensor(out=w1, in0=ps[:, 4, :], scalar=scale, in1=w1, op0=ALU.mult,
                                     op1=ALU.add).then_inc(fv, 1)
            dve.scalar_tensor_tensor(out=w2, in0=ps[:, 5, :].rearrange("p (b o) -> p b o", b=4), scalar=scale,
                                     in1=w2, op0=ALU.mult, op1=ALU.add).then_inc(fv, 1)
            dve.tensor_tensor(x1, x1, b2b.unsqueeze(1).broadcast_to([P, TT, DM]), ALU.add).then_inc(fv, 1)
            dve.wait_ge(fv, FV_XN + 3)
            for f in range(FG):
                dve.wait_ge(o_mm, f + 1)
                dve.tensor_tensor(yout[:, 4 * f:4 * f + 4, :], ps[:, 4 + f % 2, :].rearrange("p (i d) -> p i d", d=DM),
                                  x1[:, 4 * f:4 * f + 4, :], ALU.add).then_inc(o_step, 2)


_SHAPES = {"x": (T, DM), "w_in": (DM, 2 * DI + 2 * NH), "w_bc": (2, P, NQ * NH * NS), "w_out": (P, 2, DM),
           "conv_w": (P, 2, KC), "conv_b": (P, 2), "skip": (P, 2), "dt_bias": (NH,), "A_log": (NH, NS), "A_ch": (P, G),
           "w1": (DM, FF), "w2": (P, 4, DM), "b1": (P, 4), "b2": (DM,), "scale": (1,),
           "sel": (P, NH * NS), "band": (P, 60), "ident": (P, P), "causal": (P, L)}


def kernel(**inputs):
    import numpy as _np
    import concourse.bacc as _bacc
    from concourse.bass_utils import run_bass_kernel_spmd as _run

    f = {k: _np.asarray(v) for k, v in inputs.items()}
    win = f["L0_attn_W_in"]
    win = _np.concatenate([win[DI:2 * DI], win[:DI], win[2 * DI::2], win[2 * DI + 1::2]], axis=0).T
    wbc = f["L0_attn_W_bc"].reshape(G, 4, NQ, NS, 2, P).transpose(4, 5, 2, 0, 1, 3).reshape(2, P, NQ * NH * NS)

    def halves(v):
        return v.reshape((2, P) + v.shape[1:]).swapaxes(0, 1)
    rows = _np.arange(P)
    cols = _np.arange(NH * NS)
    arrays = {
        "x": f["L0_attn_x"].reshape(T, DM), "w_in": win, "w_bc": wbc,
        "w_out": f["L0_attn_W_out"].T.reshape(2, P, DM).swapaxes(0, 1),
        "conv_w": halves(f["L0_attn_dw_weight"]), "conv_b": halves(f["L0_attn_dw_bias"]),
        "skip": halves(f["L0_attn_skip"]), "dt_bias": f["L0_attn_dt_bias"], "A_log": f["L0_attn_A_log"],
        "A_ch": f["L0_attn_A_log"].reshape(G, P).T,
        "w1": f["L0_ffn_W1"].T, "w2": f["L0_ffn_W2"].T.reshape(4, P, DM).swapaxes(0, 1),
        "b1": f["L0_ffn_b1"].reshape(4, P).T, "b2": f["L0_ffn_b2"], "scale": f["L0_ffn_scale"].reshape(1),
        "sel": (rows[:, None] % NH == cols[None, :] // NS).astype(_np.float32),
        "band": (_np.arange(60)[None, :] == 28 + rows[:, None] // NS).astype(_np.float32),
        "ident": _np.eye(P, dtype=_np.float32),
        "causal": (rows[:, None] % L <= _np.arange(L)[None, :]).astype(_np.float32),
    }
    nc = _bacc.Bacc("TRN2", target_bir_lowering=False, num_devices=1)
    args, feed = {}, {}
    for name, shape in _SHAPES.items():
        arr = _np.ascontiguousarray(arrays[name])
        assert arr.shape == shape, (name, arr.shape, shape)
        feed[f"in_{name}"] = arr
        args[name] = nc.dram_tensor(f"in_{name}", shape, F32, kind="ExternalInput").ap()
    args["x4"] = nc.dram_tensor("x4_scratch", (P, T), F32, kind="Internal").ap()
    args["x4b"] = nc.dram_tensor("x4b_scratch", (3 * NH, T), BF16, kind="Internal").ap()
    args["y"] = nc.dram_tensor("out_y", (T, DM), F32, kind="ExternalOutput").ap()
    mixer_kernel(nc, args)
    r = _run(nc, [feed], core_ids=[0])
    return r.results[0]["out_y"].reshape(1, T, DM)
```

```python
from contextlib import ExitStack

import numpy as np

import concourse.bass as bass
from concourse import mybir

F32 = mybir.dt.float32
BF16 = mybir.dt.bfloat16
ALU = mybir.AluOpType
ACT = mybir.ActivationFunctionType

P = 128
T = 2048
DM = 128
DI = 256
NH = 32
NS = 32
DH = DI // NH
KC = 4
FF = 512
L = 32
TB = 256
NB = T // TB
CH = TB // L
G = NH // 4
GC = G * CH
HG = GC // 2
TT = T // P
NQ = 4
U = G * TB
LN_EPS = 1e-5
NORM_EPS = 1e-8
DT_MIN, DT_MAX, K_MAX = 1e-4, 0.1, 0.5
FG = 4
FT = T // FG


def mixer_kernel(nc, a):
    with ExitStack() as ctx:
        def sb(name, shape, dt=F32):
            return ctx.enter_context(nc.sbuf_tensor(name, shape, dt))

        def sem(name):
            return ctx.enter_context(nc.semaphore(name))

        w_in = sb("w_in", [P, 2 * DI + 2 * NH])
        w_bc = sb("w_bc", [P, 2, NQ * NH * NS])
        w_out = sb("w_out", [P, 2, DM])
        conv_w = sb("conv_w", [P, 2, KC])
        conv_b = sb("conv_b", [P, 2])
        skip = sb("skip", [P, 2])
        dt_bias = sb("dt_bias", [P, NH])
        sel3 = sb("sel3", [3 * NH, NH * NS], BF16)
        sel_in = sb("sel_in", [3 * NH, DI], BF16)
        coef = sb("coef", [P, NH * NS])
        a_ch = sb("a_ch", [P, G])
        band = sb("band", [P, 60])
        ident = sb("ident", [P, P])
        causal = sb("causal", [P, L])
        one = sb("one", [P, 1])
        junk = sb("junk", [P, 1])
        a_exp = sb("a_exp", [P, NS])
        ln_mv = sb("ln_mv", [P, TT, 2])
        ln_rstd = sb("ln_rstd", [P, TT])
        xnT = sb("xnT", [P, T])
        x1 = xnT[:, :].rearrange("p (i d) -> p i d", d=DM)
        x4 = sb("x4", [P, TB])
        xt = sb("xt", [P, 2, DM])
        raw = sb("raw", [P, NQ, GC, L])
        x4b = sb("x4b", [3 * NH, TB], BF16)
        rt = sb("rt", [P, TB])
        rt3_all = sb("rt3", [P, NQ, TB], BF16)
        rt3 = rt3_all[0:3 * NH]
        pd = sb("pd", [P, GC, L + 1])
        pi = sb("pi", [P, GC, L + 1])
        bt = sb("bt", [P, GC, L + 1])
        alpha = sb("alpha", [P, GC, L])
        rec_t = sb("rec_t", [P, 2, 2, HG])
        Z = sb("Z", [P, 2, GC, L + 1])
        S = sb("S", [P, 2, GC, L + 1])
        E = sb("E", [P, 2, GC, L])
        C = sb("C", [P, 2, GC, L])
        VR = sb("VR", [P, 2, TB + KC - 1])
        V = sb("V", [P, 2, TB])
        GS = sb("GS", [P, 2, TB])
        YG = sb("YG", [P, 2, TB])
        carry = sb("carry", [P, 2, G, DH])
        ub = sb("ub", [P, GC, L])
        vb = sb("vb", [P, 2, 2, G, 4 * DH])
        VT = E[:, 1, GC - 16:, :].rearrange("p (a c) l -> p a c l", a=2)
        psi_end = rt3_all[:, 0:2, :].rearrange("p q t -> p (q t)").bitcast(F32).rearrange(
            "p (i k g c) -> p i k g c", i=2, k=2, g=G)
        rt_hi = VR[:, 0, KC - 1:].bitcast(BF16)[:, 0:TB]
        rt_mid = VR[:, 0, KC - 1:].bitcast(BF16)[:, TB:2 * TB]
        raw_flat = raw[:, :].rearrange("p q a l -> p q (a l)")
        kraw = [raw_flat[:, 1, 512 * gh:512 * gh + 512].rearrange("p (a m) -> p a m", m=4 * DH) for gh in range(2)]
        st_t, st_z, st_s = (raw_flat[:, 1, 1024 + 128 * i:1152 + 128 * i].rearrange(
            "p (k g d) -> p k g d", k=2, g=G) for i in range(3))
        conv = raw_flat[:, 1, 1408:1920].rearrange("p (h t) -> p h t", h=2)
        kin = raw_flat[:, 2, 0:1024].rearrange("p (c k g d) -> p c k g d", c=CH, k=2, g=G)
        hist = raw_flat[:, 3, 0:1024].rearrange("p (c k g d) -> p c k g d", c=CH, k=2, g=G)
        st = [carry] + [hist[:, c] for c in range(1, CH)] + [carry]
        GM = raw[:, 0]
        ET = raw[:, 0:2]
        sq = C[:, :, HG:].rearrange("p k a b -> p k (a b)")
        VD = E[:, 1, GC - 32:GC - 16, :].rearrange("p a l -> p (a l)")
        ln_stats = VR[:, 0, KC - 1:KC - 1 + TT * 6].rearrange("p (i s) -> p i s", s=6)
        xT4 = raw[:, 0].rearrange("p a b -> p (a b)")
        xres = raw[:, 2].rearrange("p a b -> p (a b)")
        xsplit = [raw[:, 1].rearrange("p a b -> p (a b)").bitcast(BF16)[:, T * k:T * k + T] for k in range(2)]
        xsplit.append(raw[:, 3].rearrange("p a b -> p (a b)").bitcast(BF16)[:, 0:T])
        xin = E[:, 0].rearrange("p a b -> p (a b)").rearrange("p (i d) -> p i d", d=DM)
        par = C[:, :].rearrange("p a b c -> p (a b c)")[:, 0:TT * 4 * NH].rearrange("p (i k h) -> p i k h", k=4, h=NH)
        tmpf = C[:, :].rearrange("p a b c -> p (a b c)")[:, 2048:4096].rearrange("p (k i h) -> p k i h", k=4, h=NH)
        wv = w_bc[:, :, :].rearrange("p a b -> p (a b)")
        w1 = wv[:, 0:FF]
        w2 = wv[:, FF:2 * FF].rearrange("p (b o) -> p b o", b=4)
        b2b = wv[:, 1024:1152]
        b1 = wv[:, 1152:1156]
        scale = wv[:, 1156:1157]
        lt = wv[:, 1280:1280 + 16 * DM]
        hT = wv[:, 4096:4096 + 2 * 4 * FT].rearrange("p (k b t) -> p k b t", k=2, b=4)
        xn2 = Z[:, 0].rearrange("p a b -> p (a b)")[:, 0:T].rearrange("p (i d) -> p i d", d=DM)
        xn2T = S[:, 0].rearrange("p a b -> p (a b)")[:, 0:T]
        yout = C[:, 0].rearrange("p a b -> p (a b)").rearrange("p (i d) -> p i d", d=DM)

        ps = ctx.enter_context(nc.psum_tensor("ps", [P, 8, 512], F32))
        psf = ps[:, :, :].rearrange("p b c -> p (b c)")

        def slot(i):
            return psf[:, 1024 * i:1024 * i + 1024]

        def slot3(i):
            return slot(i).rearrange("p (a l) -> p a l", l=L)

        head_loaded = sem("head_loaded")
        w_loaded = sem("w_loaded")
        x_loaded = sem("x_loaded")
        xt_loaded = sem("xt_loaded")
        zeroed = sem("zeroed")
        pro = sem("pro")
        pro_act = sem("pro_act")
        pro_pe = sem("pro_pe")
        x4_stored = sem("x4_stored")
        x4_ready = sem("x4_ready")
        coef_mm = sem("coef_mm")
        d_out = sem("d_out")
        pd_ready = sem("pd_ready")
        ln_ready = sem("ln_ready")
        pi_ready = sem("pi_ready")
        newton = sem("newton")
        coef_used = sem("coef_used")
        rec_m = sem("rec_m")
        rec_a = sem("rec_a")
        val_mm = sem("val_mm")
        vr_ready = sem("vr_ready")
        gate_ready = sem("gate_ready")
        conv_step = sem("conv_step")
        tail_ready = sem("tail_ready")
        v_ready = sem("v_ready")
        vt_ready = sem("vt_ready")
        w_mm = sem("w_mm")
        sq_ready = sem("sq_ready")
        raw_ready = sem("raw_ready")
        nrm_mm = sem("nrm_mm")
        preload = sem("preload")
        root = sem("root")
        rt_step = sem("rt_step")
        rt3_ready = sem("rt3_ready")
        dtv_mm = sem("dtv_mm")
        dtv_used = sem("dtv_used")
        r_mm = sem("r_mm")
        normed = sem("normed")
        ec = sem("ec")
        ec_pool = sem("ec_pool")
        et_ready = sem("et_ready")
        psi_ready = sem("psi_ready")
        ub_zero = sem("ub_zero")
        ub_ready = sem("ub_ready")
        begun = sem("begun")
        g_mm = sem("g_mm")
        gm_ready = sem("gm_ready")
        k_mm = sem("k_mm")
        kraw_ready = sem("kraw_ready")
        kin_ready = sem("kin_ready")
        st_step = sem("st_step")
        st_ready = sem("st_ready")
        vb_ready = sem("vb_ready")
        y_mm = sem("y_mm")
        yg_step = sem("yg_step")
        out_mm = sem("out_mm")
        x1_ready = sem("x1_ready")
        ffn_w = sem("ffn_w")
        lt_moved = sem("lt_moved")
        ln2 = sem("ln2")
        root2 = sem("root2")
        turned2 = sem("turned2")
        copied2 = sem("copied2")
        outer = sem("outer")
        ffn_ready = sem("ffn_ready")
        biased = sem("biased")
        h_mm = sem("h_mm")
        h_ready = sem("h_ready")
        o_mm = sem("o_mm")
        o_step = sem("o_step")
        stored = sem("stored")

        REC = 2 * 2 * L
        EH = 9
        EC = 2 * EH
        EP = 10
        EC_OF = {(i, gh): i + EH * gh for i in range(1, EH + 1) for gh in range(2)}
        RT = 14
        ORDER = tuple((q, gh) for gh in range(2) for q in range(4))
        SLOT = (3, 3, 0, 1, 0, 1, 0, 1)
        AFTER = (0, 1, 0, 0, 3, 4, 5, 6)
        PRO_XN = 2 * TT + 2 + 1
        PRO_EXP = 2 * TT + 2 + TT + 4 + 3
        PRO_PAR = PRO_EXP + 14
        PRO_SPLIT = PRO_PAR + 8
        PRO_ACT = 1 + 4 + 4 + 4
        EARLY = TT - 2
        LN_A = 3 * EARLY + 2
        block = ctx.enter_context(nc.Block())
        head = [(w_in, a["w_in"]), (ident, a["ident"]), (coef, a["sel"]), (a_ch, a["A_ch"]), (conv_w, a["conv_w"]),
                (conv_b, a["conv_b"]), (skip, a["skip"])]
        rest = [(band, a["band"]), (causal, a["causal"]), (w_out, a["w_out"])]
        NHEAD = len(head) + 5
        NREST = len(rest) + 2

        @block.sync
        def _(sp):
            sp.dma_start(xin, a["x"].rearrange("(i p) d -> p i d", p=P)).then_inc(x_loaded, 16)
            for dst, src in head:
                full = dst[:, :] if len(dst.shape) == 2 else dst[:, :, :]
                sp.dma_start(full, src).then_inc(head_loaded, 16)
            sp.dma_start(dt_bias[:, :], a["dt_bias"].partition_broadcast(P)).then_inc(head_loaded, 16)
            for r in range(0, P, NH):
                sp.dma_start(a_exp[r:r + 32, :], a["A_log"]).then_inc(head_loaded, 16)
            for half in range(2):
                sp.dma_start(w_bc[:, half, :], a["w_bc"][half]).then_inc(w_loaded, 16)
            for dst, src in rest:
                full = dst[:, :] if len(dst.shape) == 2 else dst[:, :, :]
                sp.dma_start(full, src).then_inc(w_loaded, 16)
            xtiles = a["x"].rearrange("(b i p) d -> b p i d", i=2, p=P)

            x4_blocks, x4b_blocks = (a[n].rearrange("p (b t) -> b p t", t=TB) for n in ("x4", "x4b"))
            sp.wait_ge(pro_act, PRO_ACT - 3)
            sp.dma_start(x4[:, :], xT4[:, 0:TB]).then_inc(x4_ready, 16)
            sp.wait_ge(pro_act, PRO_ACT)
            sp.dma_start(a["x4"], xT4).then_inc(x4_stored, 16)
            sp.wait_ge(pro, PRO_SPLIT - 4)
            for k in range(3):
                sp.dma_start(x4b[NH * k:NH * k + NH, :], xsplit[k][0:NH, 0:TB]).then_inc(x4_ready, 16)
            sp.wait_ge(pro, PRO_SPLIT)
            for k in range(3):
                sp.dma_start(a["x4b"][NH * k:NH * k + NH, :], xsplit[k][0:NH, :]).then_inc(x4_stored, 16)

            def residual_rows(b):
                sp.wait_ge(x_loaded, 16)
                sp.wait_ge(x1_ready, b + 1)
                sp.dma_start(xt[:, :, :], xtiles[b]).then_inc(xt_loaded, 16)

            residual_rows(0)
            with sp.Fori(1, NB) as b:
                sp.wait_ge(x4_stored, 64)
                sp.wait_ge(rt_step, RT * b)
                sp.dma_start(x4[:, :], x4_blocks[b]).then_inc(x4_ready, 16)
                sp.dma_start(x4b[:, :], x4b_blocks[b]).then_inc(x4_ready, 16)
                residual_rows(b)
            sp.wait_ge(w_mm, 8 * NB)
            sp.dma_start(w1, a["w1"]).then_inc(ffn_w, 16)
            sp.dma_start(w2, a["w2"]).then_inc(ffn_w, 16)
            sp.dma_start(b2b, a["b2"].partition_broadcast(P)).then_inc(ffn_w, 16)
            sp.dma_start(b1, a["b1"]).then_inc(ffn_w, 16)
            sp.dma_start(scale, a["scale"].partition_broadcast(P)).then_inc(ffn_w, 16)
            sp.wait_ge(ln2, 2 * EARLY + 3)
            sp.dma_start(lt[0:1, :].rearrange("o (t d) -> o t d", d=DM), xn2[1:17, 0, :]).then_inc(lt_moved, 16)
            yd = a["y"].rearrange("(i p) d -> p i d", p=P)
            for f in range(FG):
                sp.wait_ge(o_step, 2 * (f + 1))
                sp.dma_start(yd[:, 4 * f:4 * f + 4, :], yout[:, 4 * f:4 * f + 4, :]).then_inc(stored, 16)
            sp.wait_ge(stored, 16 * FG)

        @block.tensor
        def _(pe):
            def d_rows(b):
                pe.wait_ge(x4_ready, 32 * b + 64)
                pe.wait_ge(normed, 8 * b)
                for gh in range(2):
                    for g4 in range(4):
                        g = 4 * gh + g4
                        mm = pe.matmul(slot(gh)[:, TB * g4:TB * g4 + TB], coef[:, P * g:P * g + P], x4[:, :],
                                       start=True, stop=True)
                    mm.then_inc(coef_mm, 1)

            def dt_rows(b):
                for gh in range(2):
                    pe.wait_ge(d_out, 2 * b + gh + 1)
                    for g4 in range(4):
                        g = 4 * gh + g4
                        mm = pe.matmul(slot(gh)[:, TB * g4:TB * g4 + TB], sel3[:, P * g:P * g + P], x4b[:, :],
                                       start=True, stop=True)
                    mm.then_inc(coef_mm, 1)

            def value_gate(b, k):
                if k:
                    pe.wait_ge(normed, 8 * b + 2)
                elif not isinstance(b, int) or b:
                    pe.wait_ge(normed, 8 * b - 6)
                for half in range(2):
                    col = DI * k + P * half
                    mm = pe.matmul(ps[:, 6 + k, TB * half:TB * half + TB], w_in[:, col:col + P],
                                   xnT[:, bass.ts(b, TB)], start=True, stop=True)
                mm.then_inc(val_mm, 1)

            def scale(b, k):
                q, gh = ORDER[k]
                if k in (0, 4):
                    pe.wait_ge(rt3_ready, 8 * b + k + 4)
                    pe.wait_ge(rt_step, RT * b + (7 if k == 0 else RT))
                if k == 0:
                    pe.wait_ge(dtv_used, b + 1)
                if k in (2, 3):
                    pe.wait_ge(raw_ready, 8 * b + 5 + k)
                if AFTER[k]:
                    pe.wait_ge(normed, 8 * b + AFTER[k])
                for g4 in range(4):
                    rows = P * (4 * (q % 2) + g4)
                    mm = pe.matmul(slot(SLOT[k])[:, TB * g4:TB * g4 + TB], sel3[:, rows:rows + P],
                                   rt3[:, 2 * gh + q // 2, :],
                                   start=True, stop=True)
                mm.then_inc(r_mm, 1)

            def bc_and_scales(b, between):
                def products(k):
                    gh, q = k // 4, k % 4
                    if k >= 2:
                        pe.wait_ge(raw_ready, 8 * b + k - 1)
                    for g4 in range(4):
                        col = (q * G + 4 * gh + g4) * P
                        for half in range(2):
                            mm = pe.matmul(slot(k % 2)[:, TB * g4:TB * g4 + TB], w_bc[:, half, col:col + P],
                                           V[:, half, :], start=(half == 0), stop=(half == 1))
                    mm.then_inc(w_mm, 1)

                def sums(k):
                    gh, q = k // 4, k % 4
                    pe.wait_ge(sq_ready, 8 * b + k + 1)
                    if k == 0:
                        pe.wait_ge(yg_step, 4 * b)
                    quadrant = 32 * (2 * gh + q // 2)
                    for g4 in range(4):
                        row = 16 * (q % 2) + 4 * g4
                        mm = pe.matmul(ps[quadrant:quadrant + 32, 4, 0:TB], band[:, 28 - row:60 - row],
                                       sq[:, k % 2, TB * g4:TB * g4 + TB], start=(row == 0), stop=(row == 28))
                    mm.then_inc(nrm_mm, 1)

                pe.wait_ge(gm_ready, 8 * b)
                pe.wait_ge(v_ready, 2 * b + 2)
                pe.wait_ge(coef_used, 10 * b + 10)
                for k in range(8):
                    products(k)
                    if k in between:
                        between[k]()
                    if k not in (0, 4):
                        sums(k - 1)
                    if k == 3:
                        sums(3)
                    if k == 5:
                        scale(b, 0)
                    if k == (7 if isinstance(b, int) and b == 0 else 6):
                        scale(b, 1)
                sums(7)
                for k in range(2, 4):
                    scale(b, k)

            def scores(b, gh, between={}):
                nxt = b + 2 if not isinstance(b, int) or b + 1 < NB else NB
                pe.wait_ge(ec, EC * b + EH * gh + EH)
                pe.wait_ge(ec_pool, EP * b + 5 * gh + 5)
                pe.wait_ge(kraw_ready, 2 * b + gh + 1)
                if gh == 0:
                    pe.wait_ge(normed, 8 * b + 2)
                    pe.wait_ge(x1_ready, b + 1)
                    pe.wait_ge(vr_ready, nxt)
                    pe.wait_ge(gate_ready, b + 1)
                else:
                    pe.wait_ge(gm_ready, 8 * b + 4)
                pe.sem_inc(begun, 1)
                for m in range(HG // 4):
                    if m in between:
                        between[m](b + 1)
                    for r in range(4):
                        for comp in range(2):
                            for j in range(4):
                                bank = (j + r) % 4
                                gc = HG * gh + (HG // 4) * bank + m
                                rows = slice(32 * j, 32 * j + 32)
                                mm = pe.matmul(ps[rows, 4 + bank, L * m:L * m + L], E[rows, comp, gc, :],
                                               C[rows, comp, gc, :], start=(comp == 0), stop=(comp == 1))
                mm.then_inc(g_mm, 1)

            def chunk_inputs(b, gh):
                pe.wait_ge(et_ready, 4 * b + 2 * gh + 2)
                pe.wait_ge(ub_ready, 32 * b + 32)
                if gh == 0:
                    pe.wait_ge(root, 2 * b + 2)
                else:
                    pe.wait_ge(gm_ready, 8 * b + 4)
                pe.sem_inc(begun, 1)
                for c in range(CH):
                    for comp in range(2):
                        for g4 in range(4):
                            gc = (4 * gh + g4) * CH + c
                            col = 4 * DH * (2 * c + comp)
                            mm = pe.matmul(ps[32 * g4:32 * g4 + 32, 4, col:col + 4 * DH], ET[:, comp, gc, :],
                                           ub[:, gc, :], start=True, stop=True)
                mm.then_inc(k_mm, 1)

            def outputs(b):
                pe.wait_ge(gm_ready, 8 * b + 8)
                for c in range(CH):
                    pe.wait_ge(vb_ready, 32 * b + 4 * c + 5)
                    for g in range(G):
                        gc = g * CH + c
                        out = ps[32 * (g % 4):32 * (g % 4) + 32, 4, (g // 4) * TB + c * L:(g // 4) * TB + c * L + L]
                        pe.matmul(out, ub[:, gc, :], GM[:, gc, :], start=True, stop=False)
                        pe.matmul(out, vb[:, c % 2, 0, g, :], C[:, 0, gc, :], start=False, stop=False)
                        mm = pe.matmul(out, vb[:, c % 2, 1, g, :], C[:, 1, gc, :], start=False, stop=True)
                    mm.then_inc(y_mm, 1)

            def dt_inner(b):
                for half in range(2):
                    mm = pe.matmul(ps[:, 6, TB * half:TB * half + TB], sel_in[:, P * half:P * half + P], x4b[:, :],
                                   start=True, stop=True)
                mm.then_inc(dtv_mm, 1)

            def projection(b):
                pe.wait_ge(yg_step, 4 * b + 4)
                for i in range(2):
                    for half in range(2):
                        mm = pe.matmul(ps[:, 5, DM * i:DM * i + DM], YG[:, half, P * i:P * i + P], w_out[:, half, :],
                                       start=(half == 0), stop=(half == 1))
                mm.then_inc(out_mm, 1)

            pe.wait_ge(head_loaded, 16 * NHEAD)
            for i in range(TT):
                pe.wait_ge(pro, PRO_XN + i)
                pe.transpose(psf[:, DM * i:DM * i + DM], xin[:, i, :], ident[:, :]).then_inc(pro_pe, 1)
            for i in range(TT):
                pe.wait_ge(pro_act, 1 + i // 4 + 1)
                mm = pe.matmul(psf[:, 2048 + 64 * i:2048 + 64 * i + 64], xnT[:, P * i:P * i + P],
                               w_in[:, 2 * DI:], start=True, stop=True)
            mm.then_inc(pro_pe, 1)
            pe.wait_ge(pro, PRO_PAR)
            for i in range(TT):
                mm = pe.transpose(psf[:, P * i:P * i + P], par[:, i].rearrange("p k h -> p (k h)"), ident[:, :])
            mm.then_inc(pro_pe, 1)
            pe.wait_ge(pro_act, PRO_ACT)

            def early(b):
                chunk_inputs(b, 0)
                for k in range(4, 6):
                    scale(b, k)
                value_gate(b + 1, 0)

            def last_scales(b):
                for k in range(6, 8):
                    scale(b - 1, k)

            def turn_tiles(i0, i1):
                for i in range(i0, i1):
                    pe.wait_ge(ln2, (2 * EARLY + 3 + i) if i < EARLY else (LN_A + 7 + i - EARLY))
                    pe.transpose(psf[:, DM * i:DM * i + DM], xn2[:, i, :], ident[:, :]).then_inc(turned2, 1)

            def outer_products():
                pe.wait_ge(lt_moved, 16)
                pe.wait_ge(copied2, 2)

                def token(t):
                    return lt[0:1, (t - 1) * DM:t * DM]
                for r in range(4):
                    pe.matmul(ps[:, 0, DM * r:DM * r + DM], token(2 + 2 * r), token(1 + 2 * r), start=True, stop=True)
                for r in range(4):
                    out = ps[:, 1, :].rearrange("p (q o) -> p q o", q=4)[:, :, 32 * r:32 * r + 32]
                    mm = pe.matmul(out, token(10 + 2 * r), token(9 + 2 * r).rearrange("o (k q) -> o q k", q=4),
                                   start=True, stop=True)
                mm.then_inc(outer, 1)

            value_gate(0, 0)
            d_rows(0)
            dt_rows(0)
            pe.wait_ge(w_loaded, 16 * NREST)
            bc_and_scales(0, {0: lambda: dt_inner(0)})
            value_gate(0, 1)
            early(0)
            with pe.Fori(1, NB - 1) as b:
                scores(b - 1, 0, {2: last_scales, 4: d_rows})
                dt_rows(b)
                chunk_inputs(b - 1, 1)
                scores(b - 1, 1)
                outputs(b - 1)
                bc_and_scales(b, {0: lambda: dt_inner(b)})
                value_gate(b, 1)
                projection(b - 1)
                early(b)
            scores(NB - 2, 0, {2: last_scales, 4: d_rows})
            dt_rows(NB - 1)
            chunk_inputs(NB - 2, 1)
            scores(NB - 2, 1)
            outputs(NB - 2)
            bc_and_scales(NB - 1, {0: lambda: dt_inner(NB - 1)})
            value_gate(NB - 1, 1)
            projection(NB - 2)
            chunk_inputs(NB - 1, 0)
            for k in range(4, 6):
                scale(NB - 1, k)
            scores(NB - 1, 0, {2: last_scales})
            chunk_inputs(NB - 1, 1)
            scores(NB - 1, 1)
            turn_tiles(0, EARLY)
            outputs(NB - 1)
            outer_products()
            projection(NB - 1)

            def hidden(f):
                for hb in range(4):
                    pe.wait_ge(copied2, f + 1)
                    pe.wait_ge(ffn_ready, 2)
                    k = 4 * f + hb
                    if k >= 2:
                        pe.wait_ge(h_ready, k - 1)
                    pe.matmul(ps[:, 6 + k % 2, :], w1[:, P * hb:P * hb + P], xn2T[:, FT * f:FT * f + FT],
                              start=True, stop=True).then_inc(h_mm, 1)

            def back(f):
                pe.wait_ge(h_ready, 4 * f + 4)
                if f == 0:
                    pe.wait_ge(x1_ready, NB + 1)
                if f >= 2:
                    pe.wait_ge(o_step, 2 * f - 3)
                for i in range(4):
                    for hb in range(4):
                        mm = pe.matmul(ps[:, 4 + f % 2, DM * i:DM * i + DM], hT[:, f % 2, hb, P * i:P * i + P],
                                       w2[:, hb, :], start=(hb == 0), stop=(hb == 3))
                mm.then_inc(o_mm, 1)

            hidden(0)
            for f in range(FG):
                if f == 1:
                    turn_tiles(EARLY, TT)
                if f + 1 < FG:
                    hidden(f + 1)
                back(f)

        @block.scalar
        def _(act):
            def d_copies(b):
                for gh in range(2):
                    act.wait_ge(coef_mm, 4 * b + gh + 1)
                    if gh == 0:
                        act.wait_ge(rec_a, REC * b)
                    act.activation(bt[:, HG * gh:HG * gh + HG, 1:], slot3(gh), ACT.Copy).then_inc(d_out, 1)

            def inverse_products(b):
                act.wait_ge(pd_ready, b + 1)
                act.activation(bt[:, :, 1:], pd[:, :, 1:], ACT.Ln).then_inc(ln_ready, 1)
                act.wait_ge(ln_ready, b + 1)
                act.activation(pi[:, :, 1:], bt[:, :, 1:], ACT.Exp, scale=-1.0).then_inc(pi_ready, 1)

            def values(b, gh, j):
                if gh == 0 and j == 0:
                    act.wait_ge(ub_zero, 1)
                    act.wait_ge(vt_ready, b + 1)
                for g4 in range(4):
                    gc = (4 * gh + g4) * CH
                    act.activation(ub[32 * j:32 * j + 32, gc:gc + CH, DH * j:DH * j + DH],
                                   VT[32 * g4:32 * g4 + 32, gh, :, DH * j:DH * j + DH],
                                   ACT.Copy).then_inc(ub_ready, 1)

            def values_out(b):
                act.wait_ge(val_mm, 2 * b + 1)
                act.wait_ge(tail_ready, b + 1)
                if not isinstance(b, int):
                    act.wait_ge(rt_step, RT * b)
                act.activation(VR[:, :, KC - 1:], ps[:, 6, :].rearrange("p (h t) -> p h t", h=2),
                               ACT.Copy).then_inc(vr_ready, 1)

            def front(b):
                act.wait_ge(conv_step, 8 * b + 8)
                if not isinstance(b, int):
                    act.wait_ge(yg_step, 4 * b - 2)
                for half in range(2):
                    act.activation(V[:, half, :], conv[:, half, :], ACT.Silu,
                                   bias=conv_b[:, half:half + 1]).then_inc(v_ready, 1)
                for k in range(8):
                    gh, q = k // 4, k % 4
                    act.wait_ge(w_mm, 8 * b + k + 1)
                    if k >= 2:
                        act.wait_ge(nrm_mm, 8 * b + k - 1)
                    if k == 1:
                        act.wait_ge(st_ready, 16 * b + 1)
                    act.activation(sq[:, k % 2, :], slot(k % 2), ACT.Square).then_inc(sq_ready, 1)
                    act.activation(raw[:, q, HG * gh:HG * gh + HG, :], slot3(k % 2), ACT.Copy).then_inc(raw_ready, 1)
                    if k == 1:
                        act.activation(junk[:, :], one[:, :], ACT.Sqrt).then_inc(preload, 1)
                    if k == 4:
                        scale_moves(b, 0)
                    if 1 <= k <= 6:
                        values(b, (k - 1) // 4, (k - 1) % 4)
                    if k == 3:
                        roots(b, 0)
                roots(b, 1)
                for j in range(2, 4):
                    values(b, 1, j)
                act.wait_ge(val_mm, 2 * b + 2)
                act.wait_ge(yg_step, 4 * b)
                act.activation(GS[:, :, :], ps[:, 7, :].rearrange("p (h t) -> p h t", h=2),
                               ACT.Silu).then_inc(gate_ready, 1)
                scale_moves(b, 1)

            def roots(b, part):
                act.wait_ge(nrm_mm, 8 * b + 4 * part + 4)
                rows = slice(64 * part, 64 * part + 64)
                act.activation(rt[rows, :], ps[rows, 4, 0:TB], ACT.Sqrt).then_inc(root, 1)

            def scale_moves(b, part):
                for k, src in enumerate((rt_hi, rt_mid)):
                    act.wait_ge(rt_step, RT * b + 7 * part + (3, 5)[k])
                    for q in (2 * part, 2 * part + 1):
                        act.activation(rt3[NH * k:NH * k + NH, q, :], src[NH * q:NH * q + NH, :],
                                       ACT.Copy).then_inc(rt3_ready, 1)

            def input_copy(b, gh):
                act.wait_ge(k_mm, 2 * b + gh + 1)
                act.wait_ge(ec, EC * b + EH * gh + EH)
                act.activation(kraw[gh], ps[:, 4, :].rearrange("p (a m) -> p a m", m=4 * DH),
                               ACT.Copy).then_inc(kraw_ready, 1)

            def input_moves(b, gh):
                act.wait_ge(kraw_ready, 2 * b + gh + 1)
                for j in range(4):
                    for g4 in range(4):
                        act.activation(kin[32 * j:32 * j + 32, :, :, 4 * gh + g4, :].rearrange("p c k d -> p (c k) d"),
                                       kraw[gh][32 * g4:32 * g4 + 32, :, DH * j:DH * j + DH],
                                       ACT.Copy).then_inc(kin_ready, 1)

            def spread_states(b):
                act.activation(junk[:, :], one[:, :], ACT.Silu).then_inc(preload, 1)
                for c in range(CH):
                    act.wait_ge(st_ready, 16 * b + 2 * c + 1)
                    if c >= 2:
                        act.wait_ge(y_mm, 8 * b + c - 1)
                    for j in range(4):
                        rows = slice(32 * j, 32 * j + 32)
                        act.activation(vb[rows, c % 2, :, :, DH * j:DH * j + DH], st[c][rows],
                                       ACT.Copy).then_inc(vb_ready, 1)

            act.wait_ge(pro, 2 * TT + 1)
            act.activation(ln_rstd[:, :], ln_mv[:, :, 1], ACT.Sqrt).then_inc(pro_act, 1)
            for k in range(4):
                act.wait_ge(pro_pe, 4 * k + 4)
                act.activation(xnT[:, 512 * k:512 * k + 512], ps[:, k, :], ACT.Copy).then_inc(pro_act, 1)
            act.wait_ge(head_loaded, 16 * NHEAD)
            act.activation(a_exp[:, :], a_exp[:, :], ACT.Exp).then_inc(pro_act, 1)
            act.activation(a_ch[:, :], a_ch[:, :], ACT.Exp).then_inc(pro_act, 1)
            act.wait_ge(pro, PRO_EXP)
            act.activation(tmpf[:, 0], tmpf[:, 2], ACT.Exp).then_inc(pro_act, 1)
            act.activation(tmpf[:, 1], tmpf[:, 3], ACT.Sigmoid).then_inc(pro_act, 1)
            act.wait_ge(pro_pe, TT + 2)
            for k in range(4):
                act.activation(xT4[:, 512 * k:512 * k + 512], ps[:, k, :], ACT.Copy).then_inc(pro_act, 1)
            values_out(0)
            d_copies(0)
            inverse_products(0)
            front(0)
            with act.Fori(1, NB) as b:
                input_copy(b - 1, 0)
                values_out(b)
                input_moves(b - 1, 0)
                d_copies(b)
                inverse_products(b)
                input_copy(b - 1, 1)
                spread_states(b - 1)
                front(b)
            input_copy(NB - 1, 0)
            input_moves(NB - 1, 0)
            input_copy(NB - 1, 1)
            act.wait_ge(ln2, 2 * EARLY + 1)
            act.activation(ln_rstd[:, 0:EARLY], ln_mv[:, 0:EARLY, 1], ACT.Sqrt).then_inc(root2, 1)
            spread_states(NB - 1)

            act.wait_ge(ln2, LN_A + 5)
            act.activation(ln_rstd[:, EARLY:], ln_mv[:, EARLY:, 1], ACT.Sqrt).then_inc(root2, 1)
            for k in range(4 * FG):
                f, hb = k // 4, k % 4
                act.wait_ge(h_mm, k + 1)
                if hb == 0 and f >= 2:
                    act.wait_ge(o_mm, f - 1)
                act.activation(hT[:, f % 2, hb, :], ps[:, 6 + k % 2, :], ACT.Gelu,
                               bias=b1[:, hb:hb + 1]).then_inc(h_ready, 1)

        @block.gpsimd
        def _(pool):
            def sums(b, gh):
                r = slice(HG * gh, HG * gh + HG)
                pool.wait_ge(ec, EC * b + EH * gh + 1)
                pool.tensor_tensor(E[:, 0, r], raw[:, 0, r], S[:, 1, r, 0:L], ALU.mult).then_inc(ec_pool, 1)
                pool.wait_ge(ec, EC * b + EH * gh + 3)
                pool.tensor_tensor(E[:, 1, r], C[:, 0, r], E[:, 1, r], ALU.subtract).then_inc(ec_pool, 1)
                pool.wait_ge(ec, EC * b + EH * gh + 4)
                pool.wait_ge(ec_pool, EP * b + 5 * gh + 1)
                pool.tensor_tensor(E[:, 0, r], E[:, 0, r], C[:, 1, r], ALU.subtract).then_inc(ec_pool, 1)
                pool.wait_ge(ec, EC * b + EH * gh + 6)
                pool.tensor_tensor(pi[:, r, 0:L], raw[:, 3, r], S[:, 1, r, 1:], ALU.mult).then_inc(ec_pool, 1)
                pool.wait_ge(ec, EC * b + EH * gh + 7)
                pool.tensor_tensor(C[:, 0, r], C[:, 0, r], pd[:, r, 0:L], ALU.add).then_inc(ec_pool, 1)

            def states(b):
                pool.wait_ge(kin_ready, 32 * b + 32)
                pool.wait_ge(psi_ready, 2 * b + 2)
                for c in range(CH):
                    pool.wait_ge(st_ready, 16 * b + 2 * c + 1)
                    pool.tensor_tensor(st_t[:, :], st[c][:, :], kin[:, c], ALU.add).then_inc(st_step, 1)
                    pool.wait_ge(st_step, 24 * b + 3 * c + 1)
                    for i, dst in enumerate((st_z, st_s)):
                        m = psi_end[:, i, :, :, c].unsqueeze(3).broadcast_to([P, 2, G, DH])
                        pool.tensor_tensor(dst[:, :], st_t[:, :], m, ALU.mult).then_inc(st_step, 1)
                    if c == CH - 1:
                        pool.wait_ge(vb_ready, 32 * b + 5)
                    for i, src in enumerate((st_z, st_s)):
                        pool.wait_ge(st_step, 24 * b + 3 * c + 2 + i)
                        pool.tensor_tensor(st[c + 1][:, i], src[:, 0], src[:, 1], ALU.add).then_inc(st_ready, 1)

            pool.memset(ub[:, :, :], 0.0).then_inc(ub_zero, 1)
            pool.memset(bt[:, :, 0:1], 0.0).then_inc(zeroed, 1)
            pool.memset(VR[:, :, 0:KC - 1], 0.0).then_inc(zeroed, 1)
            pool.memset(carry[:, :], 0.0).then_inc(st_ready, 1)
            pool.memset(vb[:, :], 0.0).then_inc(vb_ready, 1)
            pool.memset(Z[:, 0, :, 0:1], 1.0).then_inc(zeroed, 1)
            pool.memset(Z[:, 1, :, 0:1], 0.0).then_inc(zeroed, 1)
            pool.memset(S[:, 0, :, 0:1], 0.0).then_inc(zeroed, 1)
            pool.memset(S[:, 1, :, 0:1], 1.0).then_inc(zeroed, 1)
            pool.memset(one[:, :], 1.0).then_inc(zeroed, 1)
            pool.wait_ge(zeroed, 7)
            pool.wait_ge(pro_act, PRO_ACT)
            for gh in range(2):
                sums(0, gh)
            with pool.Fori(1, NB) as b:
                states(b - 1)
                for gh in range(2):
                    sums(b, gh)
            states(NB - 1)

        @block.vector
        def _(dve):
            def input_moves(b):
                dve.wait_ge(kraw_ready, 2 * b + 2)
                for j in range(4):
                    for g4 in range(4):
                        dve.tensor_copy(kin[32 * j:32 * j + 32, :, :, 4 + g4, :].rearrange("p c k d -> p (c k) d"),
                                        kraw[1][32 * g4:32 * g4 + 32, :, DH * j:DH * j + DH]).then_inc(kin_ready, 1)

            def coefficients(b, mask=lambda b: None):
                if not isinstance(b, int):
                    dve.wait_ge(ec_pool, EP * b)
                dve.wait_ge(d_out, 2 * b + 2)
                dve.tensor_tensor_scan(pd[:, :, :].rearrange("p a l -> p (a l)"), bt[:, :, :].rearrange("p a l -> p (a l)"),
                                       one[:, 0:1].broadcast_to([P, GC * (L + 1)]), 1.0, ALU.mult, ALU.max
                                       ).then_inc(pd_ready, 1)
                mask(b)
                dve.wait_ge(pd_ready, b + 1)
                for g in range(G):
                    r = slice(CH * g, CH * g + CH)
                    if g % 4 == 0:
                        dve.wait_ge(coef_mm, 4 * b + 3 + g // 4)
                    dve.scalar_tensor_tensor(out=alpha[:, r], in0=slot3(g // 4)[:, CH * (g % 4):CH * (g % 4) + CH],
                                             scalar=a_ch[:, g:g + 1], in1=pd[:, r, 0:L], op0=ALU.mult,
                                             op1=ALU.mult).then_inc(coef_used, 1)
                dve.wait_ge(pi_ready, b + 1)
                dve.tensor_tensor(bt[:, :, 1:], pd[:, :, 1:], pi[:, :, 1:], ALU.mult).then_inc(newton, 1)
                dve.wait_ge(newton, 2 * b + 1)
                dve.scalar_tensor_tensor(out=pi[:, :, 1:], in0=bt[:, :, 1:], scalar=2.0, in1=pi[:, :, 1:],
                                         op0=ALU.subtract, op1=ALU.mult, reverse0=True).then_inc(newton, 1)
                dve.wait_ge(newton, 2 * b + 2)
                for gh in range(2):
                    r = slice(HG * gh, HG * gh + HG)
                    dve.tensor_tensor(bt[:, r, 1:], slot3(gh), pi[:, r, 1:], ALU.mult).then_inc(coef_used, 1)

            def recursion(b, between):
                dve.wait_ge(coef_used, 10 * b + 10)
                for k in range(L):
                    if k in between:
                        between[k](b)
                    for i, (coefs, src, dst) in enumerate(((alpha[:, :, k], S[:, :, :, k], Z),
                                                           (bt[:, :, k + 1], Z[:, :, :, k + 1], S))):
                        n = 4 * k + 2 * i
                        for gh in range(2):
                            r = slice(HG * gh, HG * gh + HG)
                            if n:
                                dve.wait_ge(rec_a, REC * b + n - 2 + gh + 1)
                            m = coefs[:, r].unsqueeze(1).broadcast_to([P, 2, HG])
                            dve.tensor_tensor(rec_t[:, gh], m, src[:, :, r], ALU.mult).then_inc(rec_m, 1)
                        for gh in range(2):
                            r = slice(HG * gh, HG * gh + HG)
                            dve.wait_ge(rec_m, REC * b + n + gh + 1)
                            dve.tensor_tensor(dst[:, :, r, k + 1], dst[:, :, r, k], rec_t[:, gh],
                                              ALU.add if i else ALU.subtract).then_inc(rec_a, 1)

            def convolution(b):
                dve.wait_ge(vr_ready, b + 1)
                if not isinstance(b, int):
                    dve.wait_ge(k_mm, 2 * b)
                for half in range(2):
                    dve.tensor_scalar(conv[:, half, :], VR[:, half, 0:TB], conv_w[:, half, 0:1], None,
                                      ALU.mult).then_inc(conv_step, 1)
                for k in range(1, KC):
                    for half in range(2):
                        dve.wait_ge(conv_step, 8 * b + 2 * (k - 1) + half + 1)
                        dve.scalar_tensor_tensor(out=conv[:, half, :], in0=VR[:, half, k:k + TB],
                                                 scalar=conv_w[:, half, k:k + 1], in1=conv[:, half, :],
                                                 op0=ALU.mult, op1=ALU.add).then_inc(conv_step, 1)
                dve.wait_ge(conv_step, 8 * b + 8)
                dve.tensor_copy(VR[:, :, 0:KC - 1], VR[:, :, TB:]).then_inc(tail_ready, 1)

            def turn_values(b):
                dve.wait_ge(v_ready, 2 * b + 2)
                dve.wait_ge(dtv_mm, b + 1)
                dve.tensor_tensor(VD, V[:, :, :].rearrange("p a b -> p (a b)"), ps[:, 6, :],
                                  ALU.mult).then_inc(dtv_used, 1)
                dve.wait_ge(dtv_used, b + 1)
                dve.transpose(VT[:, :].rearrange("p a b c -> p (a b c)"), VD).then_inc(vt_ready, 1)

            def row_scales(b, part):
                dve.wait_ge(root, 2 * b + part + 1)
                rows = slice(64 * part, 64 * part + 64)
                n = RT * b + 7 * part
                dve.tensor_scalar(rt[rows, :], rt[rows, :], NORM_EPS, None, ALU.add).then_inc(rt_step, 1)
                dve.wait_ge(rt_step, n + 1)
                dve.reciprocal(rt[rows, :], rt[rows, :]).then_inc(rt_step, 1)
                dve.wait_ge(rt_step, n + 2)
                if part == 0:
                    dve.wait_ge(tail_ready, b + 2)
                    dve.wait_ge(st_ready, 16 * b + 1)
                n += 2
                dve.tensor_copy(rt_hi[rows], rt[rows, :]).then_inc(rt_step, 1)
                dve.wait_ge(rt_step, n + 1)
                dve.tensor_tensor(rt[rows, :], rt[rows, :], rt_hi[rows], ALU.subtract).then_inc(rt_step, 1)
                dve.wait_ge(rt_step, n + 2)
                dve.tensor_copy(rt_mid[rows], rt[rows, :]).then_inc(rt_step, 1)
                dve.wait_ge(rt_step, n + 3)
                for q in (2 * part, 2 * part + 1):
                    qr = slice(NH * q, NH * q + NH)
                    dve.tensor_tensor(rt3[2 * NH:3 * NH, q, :], rt[qr, :], rt_mid[qr], ALU.subtract).then_inc(rt_step, 1)

            def normed_slots(b, k0, k1):
                for k in range(k0, k1):
                    q, gh = ORDER[k]
                    r = slice(HG * gh, HG * gh + HG)
                    dve.wait_ge(r_mm, 8 * b + k + 1)
                    dve.tensor_tensor(raw[:, q, r], raw[:, q, r], slot3(SLOT[k]), ALU.mult).then_inc(normed, 1)

            def stepper(b, gh):
                def step(out, x, y, op=ALU.mult, after=0):
                    if after:
                        dve.wait_ge(ec, EC * b + EC_OF[after, gh])
                    dve.tensor_tensor(out, x, y, op).then_inc(ec, 1)
                return step

            def b_operand(b, gh):
                r = slice(HG * gh, HG * gh + HG)
                if gh == 1:
                    dve.wait_ge(ub_ready, 32 * b + 32)
                step, bz, bx = stepper(b, gh), raw[:, 0, r], raw[:, 1, r]
                if gh == 0:
                    dve.wait_ge(rec_a, REC * b + REC)
                normed_slots(b, 4 * gh, 4 * gh + 1)
                dve.wait_ge(normed, 8 * b + 4 * gh + 1)
                step(bz, bz, pd[:, r, 0:L])
                step(E[:, 1, r], bz, S[:, 0, r, 0:L], after=1)
                normed_slots(b, 4 * gh + 1, 4 * gh + 2)
                dve.wait_ge(normed, 8 * b + 4 * gh + 2)
                step(C[:, 0, r], bx, Z[:, 0, r, 1:])
                step(C[:, 1, r], bx, Z[:, 1, r, 1:])

            def turn_b(b, gh):
                r = slice(HG * gh, HG * gh + HG)
                for comp in (1, 0):
                    dve.wait_ge(ec, EC * b + EC_OF[4, gh])
                    dve.wait_ge(ec_pool, EP * b + 5 * gh + 3 - comp)
                    dve.transpose(ET[:, comp, r].rearrange("p a l -> p (a l)"),
                                  E[:, comp, r].rearrange("p a l -> p (a l)")).then_inc(et_ready, 1)

            def c_operand(b, gh, between=lambda: None):
                r = slice(HG * gh, HG * gh + HG)
                step, cz, cx = stepper(b, gh), raw[:, 2, r], raw[:, 3, r]
                p, q_, s_r, s_w = Z[:, 0, r, 1:], Z[:, 1, r, 1:], S[:, 0, r], S[:, 1, r]
                normed_slots(b, 4 * gh + 2, 4 * gh + 4)
                dve.wait_ge(normed, 8 * b + 4 * gh + 4)
                step(pd[:, r, 0:L], cx, s_r[:, :, 1:], after=1)
                step(cz, cz, pi[:, r, 1:])
                between()
                dve.wait_ge(ec_pool, EP * b + 5 * gh + 3)
                step(C[:, 0, r], cz, p, after=6)
                step(C[:, 1, r], cz, q_)
                dve.wait_ge(ec_pool, EP * b + 5 * gh + 4)
                step(C[:, 1, r], C[:, 1, r], pi[:, r, 0:L], ALU.add, after=8)
                if gh == 1:
                    dve.wait_ge(st_ready, 16 * b + 1)
                    pe2 = psi_end[:, :].rearrange("p i k g c -> p i k (g c)")
                    dve.tensor_tensor(pe2[:, 0], Z[:, :, :, L], pi[:, :, L].unsqueeze(1).broadcast_to([P, 2, GC]),
                                      ALU.mult).then_inc(psi_ready, 1)
                    dve.tensor_copy(pe2[:, 1], S[:, :, :, L]).then_inc(psi_ready, 1)

            def operands(b, after_b=lambda b: None):
                b_operand(b, 0)
                c_operand(b, 0, lambda: (turn_b(b, 0), row_scales(b, 1), after_b(b)))
                b_operand(b, 1)
                c_operand(b, 1)
                turn_b(b, 1)

            def mask_scores(b, gh):
                dve.wait_ge(g_mm, 2 * b + gh + 1)
                for i in range(4):
                    gc = HG * gh + 8 * i
                    dve.tensor_tensor(GM[:, gc:gc + 8, :], ps[:, 4 + i, 0:256].rearrange("p (a l) -> p a l", l=L),
                                      causal[:, :].unsqueeze(1).broadcast_to([P, 8, L]), ALU.mult).then_inc(gm_ready, 1)

            def skipped(b):
                for half in range(2):
                    dve.tensor_scalar(YG[:, half, :], V[:, half, :], skip[:, half:half + 1], None,
                                      ALU.mult).then_inc(yg_step, 1)

            def gated(b):
                dve.wait_ge(y_mm, 8 * b + 8)
                dve.wait_ge(yg_step, 4 * b + 2)
                flat = YG[:, :, :].rearrange("p h t -> p (h t)")
                dve.tensor_tensor(flat, flat, ps[:, 4, :], ALU.add).then_inc(yg_step, 1)
                dve.wait_ge(yg_step, 4 * b + 3)
                dve.tensor_tensor(YG[:, :, :], YG[:, :, :], GS[:, :, :], ALU.mult).then_inc(yg_step, 1)

            def residual(b):
                dve.wait_ge(out_mm, b + 1)
                dve.wait_ge(xt_loaded, 16 * b + 16)
                dve.tensor_tensor(xnT[:, bass.ts(b, TB)], ps[:, 5, 0:TB], xt[:, :, :].rearrange("p i d -> p (i d)"),
                                  ALU.add).then_inc(x1_ready, 1)

            count = [0]

            def link(ins):
                count[0] += 1
                ins.then_inc(pro, 1)
                dve.wait_ge(pro, count[0])

            dve.wait_ge(x_loaded, 16)
            for i in range(TT):
                dve.bn_stats(ln_stats[:, i, :], xin[:, i, :]).then_inc(pro, 1)
            for i in range(TT):
                dve.wait_ge(pro, i + 1)
                dve.bn_aggr(ln_mv[:, i, :], ln_stats[:, i, :]).then_inc(pro, 1)
            count[0] = 2 * TT
            dve.wait_ge(pro, 2 * TT)
            link(dve.tensor_scalar(ln_mv[:, :, 1], ln_mv[:, :, 1], LN_EPS, None, ALU.add))
            dve.wait_ge(pro_act, 1)
            link(dve.reciprocal(ln_rstd[:, :], ln_rstd[:, :]))
            for i in range(TT):
                dve.tensor_scalar(xin[:, i, :], xin[:, i, :], ln_mv[:, i, 0:1], ln_rstd[:, i:i + 1],
                                  ALU.subtract, ALU.mult).then_inc(pro, 1)
            count[0] += TT
            dve.wait_ge(head_loaded, 16 * NHEAD)
            dve.wait_ge(pro, count[0])
            dve.wait_ge(pro_act, 1 + 4 + 2)
            link(dve.tensor_copy(sel3[:, :], coef[0:96, :]))
            link(dve.tensor_copy(sel_in[:, :].rearrange("p (h d) -> p h d", d=DH),
                                 coef[0:96, :].rearrange("p (h n) -> p h n", n=NS)[:, :, 0:DH]))
            link(dve.memset(coef[0:64, :], 0.0))
            rows = slice(64, 96)
            link(dve.tensor_tensor(coef[rows, :].rearrange("p (h n) -> p h n", n=NS),
                                   coef[rows, :].rearrange("p (h n) -> p h n", n=NS),
                                   a_exp[rows, :].unsqueeze(1).broadcast_to([32, NH, NS]), ALU.mult))
            dve.wait_ge(pro_pe, TT + 1)
            pp = psf[:, 2048:3072].rearrange("p (i k h) -> p i k h", k=2, h=NH)
            dtb = dt_bias[:, :].unsqueeze(1).broadcast_to([P, TT, NH])
            link(dve.tensor_tensor(tmpf[:, 2], pp[:, :, 0], dtb, ALU.add))
            link(dve.tensor_scalar(tmpf[:, 2], tmpf[:, 2], 0.0, None, ALU.min))
            link(dve.tensor_copy(tmpf[:, 3], pp[:, :, 1]))
            assert count[0] == PRO_EXP
            dve.wait_ge(pro_act, 1 + 4 + 3)
            v, w, t2, t3 = (tmpf[:, k] for k in range(4))
            dt, dt_again, dt2, cc = (par[:, :, k] for k in range(4))
            link(dve.tensor_scalar(v, v, 0.11, None, ALU.min))
            link(dve.tensor_scalar(t2, v, 2.0, None, ALU.add))
            link(dve.reciprocal(t2, t2))
            link(dve.tensor_tensor(v, v, t2, ALU.mult))
            link(dve.tensor_tensor(t2, v, v, ALU.mult))
            dve.wait_ge(pro_act, 1 + 4 + 4)
            link(dve.tensor_scalar(t3, t2, 2.0 / 7, None, ALU.mult))
            for c, factor in ((2.0 / 5, t2), (2.0 / 3, t2), (2.0, v)):
                link(dve.scalar_tensor_tensor(out=t3, in0=t3, scalar=c, in1=factor, op0=ALU.add, op1=ALU.mult))
            link(dve.tensor_scalar(dt, t3, DT_MIN, DT_MAX, ALU.max, ALU.min))
            link(dve.tensor_copy(dt_again, dt))
            link(dve.tensor_tensor(dt2, dt, dt, ALU.mult))
            link(dve.scalar_tensor_tensor(out=w, in0=w, scalar=K_MAX, in1=dt, op0=ALU.mult, op1=ALU.mult))
            link(dve.tensor_scalar(cc, w, 1.0, None, ALU.add))
            assert count[0] == PRO_PAR, (count[0], PRO_PAR)
            for half in range(2):
                dve.wait_ge(pro_act, PRO_ACT - 2 + 2 * half)
                cols = slice(T // 2 * half, T // 2 * half + T // 2)
                hi, mid, lo = (xsplit[k][0:NH, cols] for k in range(3))
                link(dve.tensor_copy(hi, xT4[0:NH, cols]))
                link(dve.tensor_tensor(xres[0:NH, cols], xT4[0:NH, cols], hi, ALU.subtract))
                link(dve.tensor_copy(mid, xres[0:NH, cols]))
                link(dve.tensor_tensor(lo, xres[0:NH, cols], mid, ALU.subtract))
            dve.wait_ge(zeroed, 7)
            dve.tensor_copy(VR[:, :, 0:KC - 1], VR[:, :, 0:KC - 1]).then_inc(tail_ready, 1)
            dve.sem_inc(x1_ready, 1)

            own = {9: convolution, 25: turn_values, 31: lambda b: row_scales(b, 0)}
            last = {2: lambda b: input_moves(b - 1), 3: lambda b: skipped(b - 1),
                    8: lambda b: mask_scores(b - 1, 1), 17: lambda b: gated(b - 1)}
            dve.wait_ge(x4_stored, 64)
            convolution(0)
            coefficients(0)
            recursion(0, {4: turn_values, 20: own[31]})
            operands(0)
            dve.wait_ge(w_loaded, 16 * NREST)
            with dve.Fori(1, NB) as b:
                coefficients(b, lambda b: mask_scores(b - 1, 0))
                recursion(b, {**own, **last})
                operands(b, lambda b: residual(b - 1))
            def layernorm(i0, i1, n, part):
                m = i1 - i0
                for i in range(i0, i1):
                    dve.bn_stats(ln_stats[:, i, :], x1[:, i, :]).then_inc(ln2, 1)
                for i in range(i0, i1):
                    dve.wait_ge(ln2, n + i - i0 + 1)
                    dve.bn_aggr(ln_mv[:, i, :], ln_stats[:, i, :]).then_inc(ln2, 1)
                dve.wait_ge(ln2, n + 2 * m)
                dve.tensor_scalar(ln_mv[:, i0:i1, 1], ln_mv[:, i0:i1, 1], LN_EPS, None, ALU.add).then_inc(ln2, 1)
                dve.wait_ge(root2, part + 1)
                dve.reciprocal(ln_rstd[:, i0:i1], ln_rstd[:, i0:i1]).then_inc(ln2, 1)
                dve.wait_ge(ln2, n + 2 * m + 2)
                for i in range(i0, i1):
                    dve.tensor_scalar(xn2[:, i, :], x1[:, i, :], ln_mv[:, i, 0:1], ln_rstd[:, i:i + 1],
                                      ALU.subtract, ALU.mult).then_inc(ln2, 1)

            def bias(i0, i1):
                dve.wait_ge(ffn_w, 16 * 5)
                dve.wait_ge(ln2, LN_A if i0 == 0 else LN_A + 8)
                dve.tensor_tensor(x1[:, i0:i1], x1[:, i0:i1], b2b.unsqueeze(1).broadcast_to([P, i1 - i0, DM]),
                                  ALU.add).then_inc(biased, 1)

            def copy_turned(f):
                dve.wait_ge(turned2, 4 * f + 4)
                dve.tensor_copy(xn2T[:, 512 * f:512 * f + 512], ps[:, f, :]).then_inc(copied2, 1)

            mask_scores(NB - 1, 0)
            input_moves(NB - 1)
            dve.wait_ge(rt3_ready, 8 * NB)
            dve.wait_ge(ec_pool, EP * NB)
            dve.wait_ge(x1_ready, NB)
            layernorm(0, EARLY, 0, 0)
            mask_scores(NB - 1, 1)
            for f in range(FG - 1):
                copy_turned(f)
            skipped(NB - 1)
            bias(0, EARLY)
            gated(NB - 1)

            dve.wait_ge(outer, 1)
            dve.scalar_tensor_tensor(out=w1, in0=ps[:, 0, :], scalar=scale, in1=w1, op0=ALU.mult,
                                     op1=ALU.add).then_inc(ffn_ready, 1)
            dve.scalar_tensor_tensor(out=w2, in0=ps[:, 1, :].rearrange("p (b o) -> p b o", b=4), scalar=scale,
                                     in1=w2, op0=ALU.mult, op1=ALU.add).then_inc(ffn_ready, 1)
            residual(NB - 1)
            dve.wait_ge(x1_ready, NB + 1)
            layernorm(EARLY, TT, LN_A, 1)
            bias(EARLY, TT)
            copy_turned(FG - 1)
            dve.wait_ge(biased, 2)
            for f in range(FG):
                dve.wait_ge(o_mm, f + 1)
                dve.tensor_tensor(yout[:, 4 * f:4 * f + 4, :], ps[:, 4 + f % 2, :].rearrange("p (i d) -> p i d", d=DM),
                                  x1[:, 4 * f:4 * f + 4, :], ALU.add).then_inc(o_step, 2)


_SHAPES = {"x": (T, DM), "w_in": (DM, 2 * DI + 2 * NH), "w_bc": (2, P, NQ * NH * NS), "w_out": (P, 2, DM),
           "conv_w": (P, 2, KC), "conv_b": (P, 2), "skip": (P, 2), "dt_bias": (NH,), "A_log": (NH, NS), "A_ch": (P, G),
           "w1": (DM, FF), "w2": (P, 4, DM), "b1": (P, 4), "b2": (DM,), "scale": (1,),
           "sel": (P, NH * NS), "band": (P, 60), "ident": (P, P), "causal": (P, L)}


def kernel(**inputs):
    import numpy as _np
    import concourse.bacc as _bacc
    from concourse.bass_utils import run_bass_kernel_spmd as _run

    f = {k: _np.asarray(v) for k, v in inputs.items()}
    win = f["L0_attn_W_in"]
    win = _np.concatenate([win[DI:2 * DI], win[:DI], win[2 * DI::2], win[2 * DI + 1::2]], axis=0).T
    wbc = f["L0_attn_W_bc"].reshape(G, 4, NQ, NS, 2, P).transpose(4, 5, 2, 0, 1, 3).reshape(2, P, NQ * NH * NS)

    def halves(v):
        return v.reshape((2, P) + v.shape[1:]).swapaxes(0, 1)
    rows = _np.arange(P)
    cols = _np.arange(NH * NS)
    arrays = {
        "x": f["L0_attn_x"].reshape(T, DM), "w_in": win, "w_bc": wbc,
        "w_out": f["L0_attn_W_out"].T.reshape(2, P, DM).swapaxes(0, 1),
        "conv_w": halves(f["L0_attn_dw_weight"]), "conv_b": halves(f["L0_attn_dw_bias"]),
        "skip": halves(f["L0_attn_skip"]), "dt_bias": f["L0_attn_dt_bias"], "A_log": f["L0_attn_A_log"],
        "A_ch": f["L0_attn_A_log"].reshape(G, P).T,
        "w1": f["L0_ffn_W1"].T, "w2": f["L0_ffn_W2"].T.reshape(4, P, DM).swapaxes(0, 1),
        "b1": f["L0_ffn_b1"].reshape(4, P).T, "b2": f["L0_ffn_b2"], "scale": f["L0_ffn_scale"].reshape(1),
        "sel": (rows[:, None] % NH == cols[None, :] // NS).astype(_np.float32),
        "band": (_np.arange(60)[None, :] == 28 + rows[:, None] // NS).astype(_np.float32),
        "ident": _np.eye(P, dtype=_np.float32),
        "causal": (rows[:, None] % L <= _np.arange(L)[None, :]).astype(_np.float32),
    }
    nc = _bacc.Bacc("TRN2", target_bir_lowering=False, num_devices=1)
    args, feed = {}, {}
    for name, shape in _SHAPES.items():
        arr = _np.ascontiguousarray(arrays[name])
        assert arr.shape == shape, (name, arr.shape, shape)
        feed[f"in_{name}"] = arr
        args[name] = nc.dram_tensor(f"in_{name}", shape, F32, kind="ExternalInput").ap()
    args["x4"] = nc.dram_tensor("x4_scratch", (P, T), F32, kind="Internal").ap()
    args["x4b"] = nc.dram_tensor("x4b_scratch", (3 * NH, T), BF16, kind="Internal").ap()
    args["y"] = nc.dram_tensor("out_y", (T, DM), F32, kind="ExternalOutput").ap()
    mixer_kernel(nc, args)
    r = _run(nc, [feed], core_ids=[0])
    return r.results[0]["out_y"].reshape(1, T, DM)
```
